# Optimizing a Trainium2 kernel written in Bass

```python
import numpy as np
import jax
import jax.numpy as jnp

def _softmax(x, axis=-1):
    return jax.nn.softmax(x, axis=axis)

def _gelu(x):
    return jax.nn.gelu(x, approximate=True)

def _silu(x):
    return jax.nn.silu(x)

def _sigmoid(x):
    return jax.nn.sigmoid(x)

def _layernorm(x, axis=-1, eps=1e-05):
    m = jnp.mean(x, axis=axis, keepdims=True)
    v = jnp.var(x, axis=axis, keepdims=True)
    return (x - m) / jnp.sqrt(v + eps)

def _scatter_add(tgt, idx, src, axis=0):
    return tgt.at[idx].add(src)

def _segment_sum(src, seg, n):
    return jax.ops.segment_sum(src, seg, n)
kernel_name = 'mk_prb_d1_jaxref_r8_d2275f'

def setup_inputs(seed: int=0):
    np.random.seed(seed)
    _w = jnp.asarray

    def _L0_attn_setup():
        import jax, jax.numpy as jnp
        import numpy as np
        B, S, E, H = (2, 256, 128, 8)
        DH = E // H
        F = DH // 2
        key = jax.random.key(seed)
        ks = jax.random.split(key, 7)
        sc = E ** (-0.5)
        return {'x': jax.random.normal(ks[0], (B, S, E), dtype=jnp.float32), 'Wq': jax.random.normal(ks[1], (E, E), dtype=jnp.float32) * sc, 'Wk': jax.random.normal(ks[2], (E, E), dtype=jnp.float32) * sc, 'Wv': jax.random.normal(ks[3], (E, E), dtype=jnp.float32) * sc, 'norm_w': jnp.ones((H, DH), dtype=jnp.float32), 'Wo': jax.random.normal(ks[4], (E, E), dtype=jnp.float32) * sc, 'bo': jnp.zeros((E,), dtype=jnp.float32), 'diff_weight': jnp.float32(0.2)}
    _L0_attn_in = _L0_attn_setup()

    def _L0_ffn_setup():
        import jax, jax.numpy as jnp
        import numpy as np
        D_MODEL, FF_DIM = (128, 256)
        N_SHARED, N_ROUTED, TOP_K = (1, 8, 2)
        BATCH, SEQ = (2, 256)
        key = jax.random.key(seed)
        ks = jax.random.split(key, 8)
        init = lambda k, shape: jax.random.normal(k, shape, jnp.float32) * 0.02
        x = jax.random.normal(ks[0], (BATCH, SEQ, D_MODEL), jnp.float32)
        Wg = init(ks[1], (D_MODEL, N_ROUTED))
        Ws1 = init(ks[2], (D_MODEL, FF_DIM))
        Ws3 = init(ks[3], (D_MODEL, FF_DIM))
        Ws2 = init(ks[4], (FF_DIM, D_MODEL))
        We1 = init(ks[5], (N_ROUTED, D_MODEL, FF_DIM))
        We3 = init(ks[6], (N_ROUTED, D_MODEL, FF_DIM))
        We2 = init(ks[7], (N_ROUTED, FF_DIM, D_MODEL))
        return {'x': x, 'Wg': Wg, 'Ws1': Ws1, 'Ws3': Ws3, 'Ws2': Ws2, 'We1': We1, 'We3': We3, 'We2': We2}
    _L0_ffn_in = _L0_ffn_setup()
    _d = {'L0_attn_x': _L0_attn_in['x'], 'L0_attn_Wq': _L0_attn_in['Wq'], 'L0_attn_Wk': _L0_attn_in['Wk'], 'L0_attn_Wv': _L0_attn_in['Wv'], 'L0_attn_norm_w': _L0_attn_in['norm_w'], 'L0_attn_Wo': _L0_attn_in['Wo'], 'L0_attn_bo': _L0_attn_in['bo'], 'L0_attn_diff_weight': _L0_attn_in['diff_weight'], 'L0_ffn_Wg': _L0_ffn_in['Wg'], 'L0_ffn_Ws1': _L0_ffn_in['Ws1'], 'L0_ffn_Ws3': _L0_ffn_in['Ws3'], 'L0_ffn_Ws2': _L0_ffn_in['Ws2'], 'L0_ffn_We1': _L0_ffn_in['We1'], 'L0_ffn_We3': _L0_ffn_in['We3'], 'L0_ffn_We2': _L0_ffn_in['We2']}
    _x0 = _d['L0_attn_x']
    _d['L0_attn_x'] = jax.random.normal(jax.random.fold_in(jax.random.key(seed), 1), (8, 512, 128), dtype=_x0.dtype)
    del _x0
    return _d

def reference(L0_attn_x, L0_attn_Wq, L0_attn_Wk, L0_attn_Wv, L0_attn_norm_w, L0_attn_Wo, L0_attn_bo, L0_attn_diff_weight, L0_ffn_Wg, L0_ffn_Ws1, L0_ffn_Ws3, L0_ffn_Ws2, L0_ffn_We1, L0_ffn_We3, L0_ffn_We2):

    def _L0_attn_ref(x, Wq, Wk, Wv, norm_w, Wo, bo, diff_weight):
        import jax, jax.numpy as jnp
        import numpy as np
        B, S, E, H = (2, 256, 128, 8)
        DH = E // H
        F = DH // 2
        b, s, e = x.shape
        qs = (x @ Wq.T).reshape(b, s, H, 2, F)
        ks_ = (x @ Wk.T).reshape(b, s, H, 2, F)
        vs = (x @ Wv.T).reshape(b, s, H, DH)
        scale = F ** (-0.5)
        scores = jnp.einsum('bqhif,bkhif->ibhqk', qs, ks_) * scale
        atts = jax.nn.softmax(scores, axis=-1)
        att = atts[0] - diff_weight * atts[1]
        o = jnp.einsum('bhqk,bkhe->bqhe', att, vs)
        eps = jnp.finfo(o.dtype).eps
        rms = jax.lax.rsqrt(jnp.mean(o * o, axis=(-2, -1), keepdims=True) + eps)
        normed = (o * rms * norm_w).reshape(b, s, e)
        return (normed @ Wo.T + bo) * (1.0 - diff_weight)

    def _L0_ffn_ref(x, Wg, Ws1, Ws3, Ws2, We1, We3, We2):
        import jax, jax.numpy as jnp
        import numpy as np
        D_MODEL, FF_DIM = (128, 256)
        N_SHARED, N_ROUTED, TOP_K = (1, 8, 2)
        BATCH, SEQ = (2, 256)
        B, S, d = x.shape
        E = Wg.shape[1]
        xf = x.reshape(-1, d)
        T = xf.shape[0]
        gates = jax.nn.sigmoid(xf @ Wg)
        vals, idx = jax.lax.top_k(gates, TOP_K)
        vals = vals / vals.sum(axis=-1, keepdims=True)
        w = jnp.zeros((T, E), x.dtype).at[jnp.arange(T)[:, None], idx].add(vals)
        shared = jax.nn.silu(xf @ Ws1) * (xf @ Ws3) @ Ws2
        h = jax.nn.silu(jnp.einsum('td,edf->tef', xf, We1)) * jnp.einsum('td,edf->tef', xf, We3)
        routed = jnp.einsum('tef,efd,te->td', h, We2, w)
        out = (shared + routed) / (N_SHARED + TOP_K)
        return out.reshape(B, S, d)
    x = L0_attn_x
    xn = _layernorm(x, axis=-1)
    x = x + _L0_attn_ref(xn, L0_attn_Wq, L0_attn_Wk, L0_attn_Wv, L0_attn_norm_w, L0_attn_Wo, L0_attn_bo, L0_attn_diff_weight) + _L0_ffn_ref(xn, L0_ffn_Wg, L0_ffn_Ws1, L0_ffn_Ws3, L0_ffn_Ws2, L0_ffn_We1, L0_ffn_We3, L0_ffn_We2)
    return x

_drawn_inputs = setup_inputs


def setup_inputs(seed=0):
    import zlib

    import numpy as np

    out = dict(_drawn_inputs(seed))
    spreads = {'L0_attn_norm_w': (1.0, 0.2), 'L0_attn_bo': (0.0, 0.1)}
    factors = {'L0_ffn_Wg': 8.0,
     'L0_ffn_Ws1': 8.0,
     'L0_ffn_Ws3': 8.0,
     'L0_ffn_Ws2': 8.0,
     'L0_ffn_We1': 8.0,
     'L0_ffn_We3': 8.0,
     'L0_ffn_We2': 8.0}
    for name, (base, spread) in spreads.items():
        noise = np.random.default_rng([zlib.crc32(name.encode()), seed]).standard_normal(out[name].shape)
        drawn = base * np.exp(spread * noise) if base else spread * noise
        out[name] = jnp.asarray(drawn.astype(out[name].dtype))
    for name, factor in factors.items():
        out[name] = (out[name] * factor).astype(out[name].dtype)
    return out
```

```python
import concourse.bass as bass
from concourse import mybir
from contextlib import ExitStack


def differential_attention_moe_block(
    nc: bass.Bass,
    x_in: bass.AP,
    Wq: bass.AP,
    Wk: bass.AP,
    Wv: bass.AP,
    norm_w: bass.AP,
    Wo: bass.AP,
    bo: bass.AP,
    diff_weight: bass.AP,
    Wg: bass.AP,
    Ws1: bass.AP,
    Ws3: bass.AP,
    Ws2: bass.AP,
    We1: bass.AP,
    We3: bass.AP,
    We2: bass.AP,
    out: bass.AP,
):
    f32 = mybir.dt.float32
    f32r = mybir.dt.float32r
    bf16 = mybir.dt.bfloat16
    ALU = mybir.AluOpType
    ACT = mybir.ActivationFunctionType
    AX = mybir.AxisListType.X

    BATCH, SEQ, D = x_in.shape
    H, DH = norm_w.shape
    MAPS = 2
    FD = DH // MAPS
    HM = H * MAPS
    E = We1.shape[0]
    FF = We1.shape[2]
    TOPK, SHARED = 2, 1
    P = 128
    QT = SEQ // P
    PARTS = 3
    TERMS = PARTS * PARTS * FD
    ROWS = TERMS + PARTS
    SCALE = float(FD) ** -0.5
    LN_EPS = 1e-5
    RMS_EPS = 2.0 ** -23
    GROUPS = HM // 4
    TILES = HM * QT
    UNITS = HM * QT // 2
    VW = 32
    NP = 8
    NHB = 4
    FC = FF // P
    CH = (E + SHARED) * FC
    RCH = E * FC
    NWB = 2
    LAG = 3
    LN_STEPS, TOP_STEPS, MS_STEPS, OE_STEPS = 7, 19, 5, 4 * QT + 4

    q_scr = nc.dram_tensor("q_scr", (2, PARTS, P, SEQ), bf16, kind="Internal").ap()
    k_scr = nc.dram_tensor("k_scr", (2, 2 * PARTS - 1, P, SEQ), bf16, kind="Internal").ap()
    m_scr = nc.dram_tensor("m_scr", (2, PARTS, HM, SEQ), bf16, kind="Internal").ap()
    w_scr = nc.dram_tensor("w_scr", (2, E * SEQ), f32, kind="Internal").ap()

    ctx = ExitStack()
    with ctx:
        def sb(name, shape, dt=f32):
            return ctx.enter_context(nc.sbuf_tensor(name, shape, dt))

        def pb(name, shape):
            return ctx.enter_context(nc.psum_tensor(name, shape, f32))

        def sem(name):
            return ctx.enter_context(nc.semaphore(name))

        ident = sb("ident", [P, P])
        ident_b = sb("ident_b", [P, P], bf16)
        wqkvT = sb("wqkvT", [P, 3, P])
        woT = sb("woT", [P, P])
        nw_col = sb("nw_col", [P, 1])
        bo_col = sb("bo_col", [P, 1])
        dw_col = sb("dw_col", [P, 1])
        ndw = sb("ndw", [P, 1])
        omd = sb("omd", [P, 1])
        wos = sb("wos", [P, 1])
        bos = sb("bos", [P, 1])
        wg = sb("wg", [P, E])
        w13h = sb("w13h", [P, E + SHARED, 2 * FF], f32r)
        w13l = sb("w13l", [P, E + SHARED, 2 * FF], f32r)
        w2 = sb("w2", [P, E + SHARED, FC, D])
        half = sb("half", [P, QT])
        one = sb("one", [P, 1])
        scrap = sb("scrap", [P, 1])
        rank = sb("rank", [P, QT, E])
        xin = sb("xin", [P, QT, D])
        xc = sb("xc", [P, QT, D])
        sq = sb("sq", [P, QT, D])
        xn = sb("xn", [P, QT, D])
        ln_s = sb("ln_s", [P, 6, QT])
        xT = sb("xT", [P, SEQ])
        xh = [sb(f"xh{i}", [P, SEQ], f32r) for i in range(2)]
        xl = [sb(f"xl{i}", [P, SEQ], f32r) for i in range(2)]
        qparts = sb("qparts", [P, PARTS, SEQ], bf16)
        kparts = sb("kparts", [P, PARTS, SEQ], bf16)
        qres = sb("qres", [P, SEQ])
        kres = sb("kres", [P, SEQ])
        qop = [sb(f"qop{i}", [ROWS, HM, SEQ], bf16) for i in range(2)]
        kop = [sb(f"kop{i}", [ROWS, HM, SEQ], bf16) for i in range(2)]
        vop = [sb(f"vop{i}", [P, QT, H, VW]) for i in range(2)]
        rowmax = sb("rowmax", [P, HM, QT])
        mpad = sb("mpad", [P, QT, P], bf16)
        mparts = mpad[:, :, 0:PARTS * HM].rearrange("p t (a m) -> p t a m", a=PARTS)
        mres = sb("mres", [P, QT, 2, HM])
        mrows = sb("mrows", [PARTS * HM, SEQ], bf16)
        probs = sb("probs", [P, NP, SEQ])
        oT = sb("oT", [P, GROUPS, SEQ])
        o_inv = sb("o_inv", [P, HM])
        o_sc = sb("o_sc", [P, HM, DH])
        o_n = sb("o_n", [P, QT, D])
        o_st = sb("o_st", [P, 2, QT])
        nT = sb("nT", [P, SEQ])
        zg = sb("zg", [P, QT, E])
        eg = sb("eg", [P, QT, E])
        tk = sb("tk", [P, 10, QT, E])
        tks = sb("tks", [P, 8, QT])
        rw = sb("rw", [P, QT, E])
        rwT = sb("rwT", [E, SEQ])
        rwb = sb("rwb", [P, E, SEQ])
        sil = sb("sil", [P, 2, SEQ])
        w13 = sil
        hid = probs[:, 0:NHB, :]
        hidw = probs[:, NHB:2 * NHB, :]
        yT = nT
        res = sb("res", [P, QT, D])
        w_raw = res

        S = [pb(f"S{i}", [P, 2, SEQ]) for i in range(2)]
        ST = [pb(f"ST{i}", [P, SEQ]) for i in range(3)]
        O = pb("O", [P, SEQ])

        s_wraw, s_small, s_wbig = sem("w_raw_loaded"), sem("small_loaded"), sem("w_big_loaded")
        s_id, s_wT, s_wTc, s_const = sem("ident_set"), sem("wT_ready"), sem("wT_copied"), sem("const_steps")
        s_half, s_pad, s_v0, s_w13, s_kone = sem("half_set"), sem("pad_set"), sem("v_set"), sem("w13_split"), sem("k_ones_set")
        s_w13l = [sem(f"w13_loaded{n}") for n in range(NWB)]
        s_woT, s_w2s = sem("woT_ready"), sem("w2_scaled")
        s_xin, s_ln, s_xT, s_xTc, s_xs = sem("x_loaded"), sem("ln_steps"), sem("xT_ready"), sem("xT_copied"), sem("x_split")
        s_q, s_k, s_v, s_g = sem("q_ready"), sem("k_ready"), sem("v_ready"), sem("g_ready")
        s_q1, s_k1, s_vc, s_z = sem("q1_ready"), sem("k1_ready"), sem("v_copied"), sem("z_copied")
        s_qr, s_kr, s_q3, s_k3 = sem("q_res"), sem("k_res"), sem("q_split"), sem("k_split")
        s_qst, s_kst, s_ql, s_kl = sem("q_stored"), sem("k_stored"), [sem("q_loaded0"), sem("q_loaded1")], [sem("k_loaded0"), sem("k_loaded1")]
        s_eg, s_tk, s_rwT, s_rwc = sem("gate_exp"), sem("top_steps"), sem("rwT_ready"), sem("rwT_copied")
        s_rws, s_rwb = sem("rw_stored"), sem("rw_loaded")
        s_s, s_mx, s_ms, s_mT, s_mc = sem("s_ready"), sem("max_ready"), sem("max_split"), sem("mT_ready"), sem("m_copied")
        s_mst, s_ml = sem("m_stored"), sem("m_loaded")
        s_st, s_p, s_av, s_oe = sem("st_ready"), sem("probs_ready"), sem("av_done"), sem("o_copied")
        s_ot, s_on, s_nT, s_nc = sem("oT_ready"), sem("o_steps"), sem("nT_ready"), sem("nT_copied")
        s_h1, s_h3, s_si, s_hm, s_hw = sem("h1_ready"), sem("h3_ready"), sem("silu_ready"), sem("hid_ready"), sem("hidw_ready")
        s_y, s_wo, s_yc, s_u = sem("down_done"), sem("y_ready"), sem("y_copied"), sem("u_ready")
        s_rs, s_rp = sem("ln_pow"), sem("rms_pow")
        s_rank, s_warm = sem("rank_set"), sem("table_warm")
        s_xr, s_out, s_ost = sem("xres_loaded"), sem("res_ready"), sem("out_stored")

        block = ctx.enter_context(nc.Block())

        def batches(eng, attend, ffn):
            attend(0, 0, more=True, behind=False)
            with eng.Fori(0, BATCH // 2 - 1) as i:
                for par in range(2):
                    ffn(2 * i + par, par, more=True, prep=True)
                    attend(2 * i + par + 1, 1 - par, more=True, behind=True)
            ffn(BATCH - 2, 0, more=True, prep=False)
            attend(BATCH - 1, 1, more=False, behind=True)
            ffn(BATCH - 1, 1, more=False, prep=False)

        @block.sync
        def _(sp):
            sp.dma_start(xin[:, :, :], x_in[0].rearrange("(t p) d -> p t d", p=P)).then_inc(s_xin, 16)
            for j, w in enumerate((Wq, Wk, Wv, Wo)):
                sp.dma_start(w_raw[:, j, :], w).then_inc(s_wraw, 16)
            sp.dma_start(nw_col[:, :], norm_w.rearrange("h (e o) -> (h e) o", o=1)).then_inc(s_small, 16)
            sp.dma_start(bo_col[:, :], bo.rearrange("(d o) -> d o", o=1)).then_inc(s_small, 16)
            sp.dma_start(dw_col[:, :], diff_weight.partition_broadcast(P)).then_inc(s_small, 16)
            sp.dma_start(wg[:, :], Wg).then_inc(s_small, 16)
            sp.dma_start(w2[:, 0, :, :], Ws2.rearrange("(c f) d -> f c d", f=P)).then_inc(s_wbig, 16)
            for c in range(FC):
                sp.dma_start(w2[:, 1:, c, :], We2[:, c * P:(c + 1) * P, :].rearrange("e f d -> f e d"))\
                  .then_inc(s_wbig, 16)

            def load_x(x):
                sp.wait_ge(s_ln, LN_STEPS * x)
                sp.dma_start(xin[:, :, :], x_in[x].rearrange("(t p) d -> p t d", p=P)).then_inc(s_xin, 16)

            def lay_qk(x, par):
                sp.wait_ge(s_q3, 3 * x + 3)
                sp.dma_start(q_scr[par].rearrange("a p t -> p a t"), qparts[:, :, :]).then_inc(s_qst, 16)
                sp.wait_ge(s_k3, 3 * x + 3)
                sp.dma_start(k_scr[par, 0:PARTS].rearrange("a p t -> p a t"), kparts[:, :, :]).then_inc(s_kst, 16)
                sp.dma_start(k_scr[par, PARTS:].rearrange("a p t -> p a t"), kparts[:, 0:PARTS - 1, :])\
                  .then_inc(s_kst, 16)
                R = PARTS * FD
                sp.wait_ge(s_qst, 16 * x + 16)
                for r in range(PARTS):
                    sp.dma_start(qop[par][r * R:(r + 1) * R, :, :],
                                 q_scr[par].rearrange("a (f m) t -> (a f) m t", m=HM)).then_inc(s_ql[par], 16)
                sp.wait_ge(s_kst, 32 * x + 32)
                for r in range(PARTS):
                    sp.dma_start(kop[par][r * R:(r + 1) * R, :, :],
                                 k_scr[par, r:r + PARTS].rearrange("a (f m) t -> (a f) m t", m=HM))\
                      .then_inc(s_kl[par], 16)

            def lay_m(x, par):
                sp.wait_ge(s_mc, x + 1)
                sp.dma_start(m_scr[par].rearrange("a m t -> (a m) t"), mrows[:, :]).then_inc(s_mst, 16)
                sp.wait_ge(s_mst, 16 * x + 16)
                sp.dma_start(qop[par][TERMS:ROWS, :, :], m_scr[par]).then_inc(s_ml, 16)

            def store_rw(x, par):
                sp.wait_ge(s_rwc, x + 1)
                sp.dma_start(w_scr[par].rearrange("(e t) -> e t", e=E), rwT[:, :]).then_inc(s_rws, 16)

            def load_rw(x, par):
                sp.wait_ge(s_rws, 16 * x + 16)
                sp.wait_ge(s_hw, RCH * x)
                sp.dma_start(rwb[:, :, :].rearrange("p e t -> p (e t)"), w_scr[par].partition_broadcast(P))\
                  .then_inc(s_rwb, 16)

            def load_res(b):
                sp.dma_start(res[:, :, :], x_in[b].rearrange("(t p) d -> p t d", p=P)).then_inc(s_xr, 16)

            load_x(1)
            sp.wait_ge(s_kone, 1)
            lay_qk(0, 0)
            sp.wait_ge(s_kone, 2)
            lay_qk(1, 1)
            lay_m(0, 0)
            store_rw(0, 0)
            load_rw(0, 0)
            sp.wait_ge(s_wT, 1)
            load_res(0)

            def store_out(b):
                sp.wait_ge(s_out, b + 1)
                sp.dma_start(out[b].rearrange("(t p) d -> p t d", p=P), res[:, :, :]).then_inc(s_ost, 16)

            def attend(b, par, more, behind):
                if behind:
                    store_out(b - 1)
                    sp.wait_ge(s_ost, 16 * b)
                    load_res(b)

            def ffn(b, par, more, prep):
                if prep:
                    load_x(b + 2)
                if more:
                    store_rw(b + 1, 1 - par)
                    lay_m(b + 1, 1 - par)
                if prep:
                    sp.wait_ge(s_st, TILES * (b + 1))
                    lay_qk(b + 2, par)
                if more:
                    load_rw(b + 1, 1 - par)

            batches(sp, attend, ffn)
            store_out(BATCH - 1)
            sp.wait_ge(s_ost, 16 * BATCH)

        @block.gpsimd
        def _(gp):
            nc.gpsimd.memset(half[:, :], -0.5).then_inc(s_half, 1)
            nc.gpsimd.memset(one[:, :], 1.0).then_inc(s_half, 1)
            nc.gpsimd.memset(ident[:, :], 0.0).then_inc(s_id, 1)
            nc.gpsimd.memset(ident_b[:, :], 0.0).then_inc(s_id, 1)
            gp.wait_ge(s_id, 2)
            for m in (ident, ident_b):
                nc.gpsimd.affine_select(out=m[:, :], in_=m[:, :], compare_op=ALU.not_equal, fill=1.0, base=0,
                                        pattern=[[-1, P]], channel_multiplier=1).then_inc(s_id, 1)

            def split(x, s_res, s_parts, parts, r, s_stored, n_stored):
                gp.wait_ge(s_res, x + 1)
                nc.gpsimd.tensor_tensor(parts[:, 1, :], r[:, :], ones, ALU.mult).then_inc(s_parts, 1)
                gp.wait_ge(s_parts, 3 * x + 1)
                nc.gpsimd.tensor_tensor(r[:, :], r[:, :], parts[:, 1, :], ALU.subtract).then_inc(s_parts, 1)
                gp.wait_ge(s_parts, 3 * x + 2)
                nc.gpsimd.tensor_tensor(parts[:, 2, :], r[:, :], ones, ALU.mult).then_inc(s_parts, 1)

            def split_q(x):
                split(x, s_qr, s_q3, qparts, qres, s_qst, 16)

            def split_k(x):
                split(x, s_kr, s_k3, kparts, kres, s_kst, 32)

            def split_x(x, par):
                gp.wait_ge(s_xTc, x + 1)
                nc.gpsimd.tensor_tensor(xh[par][:, :], xT[:, :], ones, ALU.mult).then_inc(s_xs, 1)
                gp.wait_ge(s_xs, 2 * x + 1)
                nc.gpsimd.tensor_tensor(xl[par][:, :], xT[:, :], xh[par][:, :].bitcast(f32), ALU.subtract)\
                  .then_inc(s_xs, 1)

            def load_w13(e):
                for side, (ws, we) in enumerate(((Ws1, We1), (Ws3, We3))):
                    gp.dma_start(w13[:, e % NWB, side * FF:(side + 1) * FF], we[e - SHARED] if e else ws)\
                      .then_inc(s_w13l[e % NWB], 16)

            gp.wait_ge(s_half, 2)
            ones = one[:, :].to_broadcast([P, SEQ])

            def norm_pow(x):
                gp.wait_ge(s_ln, LN_STEPS * x + 6)
                nc.gpsimd.tensor_tensor(ln_s[:, 4, :], ln_s[:, 3, :], half[:, :], ALU.pow).then_inc(s_rs, 1)

            def rms_pow(b):
                gp.wait_ge(s_on, OE_STEPS * b + 4 * QT + 3)
                nc.gpsimd.tensor_tensor(o_st[:, 0, :], o_st[:, 1, :], half[:, :], ALU.pow).then_inc(s_rp, 1)

            norm_pow(0)
            for e in range(NWB):
                load_w13(e)
            for i in range(2):
                nc.gpsimd.memset(vop[i][:, :, :, :], 0.0).then_inc(s_v0, 1)
            gp.wait_ge(s_v0, 2)
            for i in range(2):
                nc.gpsimd.memset(vop[i][:, :, :, DH:DH + 1], 1.0).then_inc(s_v0, 1)
            nc.gpsimd.memset(mpad[:, :, :], 0.0).then_inc(s_pad, 1)
            split_q(0)
            split_k(0)
            split_x(0, 0)
            norm_pow(1)
            split_q(1)
            split_k(1)
            split_x(1, 1)
            gp.wait_ge(s_wbig, 16 * (1 + FC))
            nc.gpsimd.tensor_scalar(w2[:, 0, :, :], w2[:, 0, :, :], 1.0 / (SHARED + TOPK), None, ALU.mult)\
              .then_inc(s_w2s, 1)
            for e in range(E + SHARED):
                gp.wait_ge(s_w13l[e % NWB], 32 * (e // NWB + 1))
                nc.gpsimd.tensor_copy(w13h[:, e, :], w13[:, e % NWB, :]).then_inc(s_w13, 1)
                gp.wait_ge(s_w13, 2 * e + 1)
                nc.gpsimd.tensor_tensor(w13l[:, e, :], w13[:, e % NWB, :], w13h[:, e, :].bitcast(f32), ALU.subtract)\
                  .then_inc(s_w13, 1)
                if e + NWB < E + SHARED:
                    gp.wait_ge(s_w13, 2 * e + 2)
                    load_w13(e + NWB)

            def attend(b, par, more, behind):
                pass

            def ffn(b, par, more, prep):
                gp.wait_ge(s_rwb, 16 * b + 16)
                for c in range(CH):
                    if c >= SHARED * FC:
                        gp.wait_ge(s_hm, CH * b + c + 1)
                        if c >= NHB:
                            gp.wait_ge(s_y, CH * b + c - NHB + 1)
                        nc.gpsimd.tensor_tensor(hidw[:, c % NHB, :], hid[:, c % NHB, :],
                                                rwb[:, c // FC - SHARED, :], ALU.mult).then_inc(s_hw, 1)
                    if prep and c == 6:
                        norm_pow(b + 2)
                    if c == 10:
                        rms_pow(b)
                    if prep and c == 11:
                        split_q(b + 2)
                    if prep and c == 12:
                        split_k(b + 2)
                if prep:
                    gp.wait_ge(s_h3, CH * (b + 1))
                    split_x(b + 2, par)

            batches(gp, attend, ffn)

        @block.scalar
        def _(act):
            def copy_xT(x):
                act.wait_ge(s_xT, x + 1)
                if x is not 0:
                    act.wait_ge(s_xs, 2 * x)
                    act.wait_ge(s_g, x)
                nc.scalar.activation(xT[:, :], ST[XT_BANK(x)][:, :], ACT.Copy).then_inc(s_xTc, 1)

            def XT_BANK(x):
                return 1 if x is 0 or x is 1 else 0

            def Q_BANK(x):
                return 2 if x is 0 or x is 1 else 1

            def K_BANK(x):
                return 0 if x is 0 or x is 1 else 2

            def copy_q(x):
                act.wait_ge(s_q, x + 1)
                if x is not 0:
                    act.wait_ge(s_qst, 16 * x)
                nc.scalar.activation(qparts[:, 0, :], ST[Q_BANK(x)][:, :], ACT.Copy).then_inc(s_q1, 1)

            def copy_k(x):
                act.wait_ge(s_k, x + 1)
                if x is not 0:
                    act.wait_ge(s_kst, 32 * x)
                nc.scalar.activation(kparts[:, 0, :], ST[K_BANK(x)][:, :], ACT.Copy).then_inc(s_k1, 1)

            def copy_v(x, par):
                act.wait_ge(s_v, x + 1)
                nc.scalar.activation(vop[par][:, :, :, 0:DH],
                                     ST[XT_BANK(x)][:, :].rearrange("p (t h e) -> p t h e", t=QT, h=H),
                                     ACT.Copy).then_inc(s_vc, 1)

            def copy_z(x):
                act.wait_ge(s_g, x + 1)
                nc.scalar.activation(zg[:, :, :].rearrange("p t e -> p (t e)"), ST[Q_BANK(x)][:, 0:QT * E], ACT.Copy)\
                   .then_inc(s_z, 1)

            def gate_exp(x):
                act.wait_ge(s_z, x + 1)
                act.wait_ge(s_tk, TOP_STEPS * x)
                nc.scalar.activation(eg[:, :, :], zg[:, :, :], ACT.Exp, scale=-1.0).then_inc(s_eg, 1)

            def copy_rwT(x, bank=0):
                act.wait_ge(s_rwT, x + 1)
                act.wait_ge(s_rws, 16 * x)
                nc.scalar.activation(rwT[:, :], ST[bank][0:E, :], ACT.Copy).then_inc(s_rwc, 1)

            def copy_m(x, bank):
                act.wait_ge(s_mT, x + 1)
                act.wait_ge(s_mst, 16 * x)
                nc.scalar.activation(mrows[:, :], ST[bank][0:PARTS * HM, 0:SEQ // 2].bitcast(bf16), ACT.Copy)\
                   .then_inc(s_mc, 1)

            act.wait_ge(s_wT, 1)
            for j in range(2):
                nc.scalar.activation(wqkvT[:, j, :].rearrange("p (f m) -> p m f", m=HM),
                                     ST[0][:, j * P:(j + 1) * P].rearrange("p (m f) -> p m f", m=HM),
                                     ACT.Copy).then_inc(s_wTc, 1)
            nc.scalar.activation(wqkvT[:, 2, :], ST[0][:, 2 * P:3 * P], ACT.Copy).then_inc(s_wTc, 1)
            copy_xT(0)
            copy_q(0)
            copy_k(0)
            act.wait_ge(s_v0, 4)
            copy_v(0, 0)
            copy_z(0)
            gate_exp(0)
            copy_xT(1)
            copy_q(1)
            copy_k(1)
            copy_v(1, 1)
            copy_z(1)
            copy_m(0, 0)
            copy_rwT(0, 1)

            def warm(func):
                nc.scalar.activation(scrap[:, :], bos[:, 0:1], func).then_inc(s_warm, 1)

            def attend(b, par, more, behind):
                for s in range(TILES):
                    act.wait_ge(s_st, TILES * b + s + 1)
                    if s >= NP:
                        act.wait_ge(s_av, TILES * b + s - NP + 1)
                    nc.scalar.activation(probs[:, s % NP, :], ST[s % 3][:, :], ACT.Exp, scale=SCALE).then_inc(s_p, 1)
                    if more and s == 2:
                        gate_exp(b + 1)
                    if s % 16 == 5 and s > 16:
                        copy_o(b, s // 16 - 1)
                copy_o(b, GROUPS - 1)
                warm(ACT.Silu)

            def copy_o(b, g):
                act.wait_ge(s_av, TILES * b + 16 * (g + 1))
                nc.scalar.activation(oT[:, g, :], O[:, :], ACT.Copy).then_inc(s_oe, 1)

            def ffn(b, par, more, prep):
                for c in range(CH):
                    act.wait_ge(s_h1, CH * b + c + 1)
                    if c >= 2:
                        act.wait_ge(s_hm, CH * b + c - 1)
                    nc.scalar.activation(sil[:, c % 2, :], S[c % 2][:, 0, :], ACT.Silu).then_inc(s_si, 1)
                    if more and c == 0:
                        copy_rwT(b + 1)
                    if more and c == 2:
                        copy_m(b + 1, 1)
                    if prep:
                        if c == 9:
                            copy_xT(b + 2)
                        if c == 10:
                            copy_q(b + 2)
                        if c == 11:
                            copy_k(b + 2)
                        if c == 12:
                            copy_v(b + 2, par)
                        if c == 13:
                            copy_z(b + 2)
                    if c == 14:
                        act.wait_ge(s_nT, b + 1)
                        nc.scalar.activation(nT[:, :], ST[2][:, :], ACT.Copy).then_inc(s_nc, 1)
                warm(ACT.Exp)
                act.wait_ge(s_wo, b + 1)
                nc.scalar.activation(yT[:, :], O[:, :], ACT.Identity, bias=bos[:, 0:1]).then_inc(s_yc, 1)

            batches(act, attend, ffn)

        @block.vector
        def _(dve):
            V = nc.vector

            def step(ins, s, n):
                ins.then_inc(s, 1)
                dve.wait_ge(s, n)

            def per_tile(col, width):
                return col.unsqueeze(2).to_broadcast([P, col.shape[1], width])

            def norm_steps(x):
                at = LN_STEPS * x

                def first():
                    dve.wait_ge(s_xin, 16 * x + 16)
                    step(V.reduce_sum(ln_s[:, 0, :], xin[:, :, :], AX), s_ln, at + 1)
                    step(V.tensor_scalar(ln_s[:, 1, :], ln_s[:, 0, :], -1.0 / D, None, ALU.mult), s_ln, at + 2)
                    step(V.tensor_tensor(xc[:, :, :], xin[:, :, :], per_tile(ln_s[:, 1, :], D), ALU.add), s_ln, at + 3)

                def second():
                    step(V.tensor_tensor(sq[:, :, :], xc[:, :, :], xc[:, :, :], ALU.mult), s_ln, at + 4)
                    step(V.reduce_sum(ln_s[:, 2, :], sq[:, :, :], AX), s_ln, at + 5)
                    step(V.tensor_scalar(ln_s[:, 3, :], ln_s[:, 2, :], 1.0 / D, LN_EPS, ALU.mult, ALU.add), s_ln, at + 6)

                def third():
                    dve.wait_ge(s_rs, x + 1)
                    if x is not 0:
                        dve.wait_ge(s_xT, x)
                    step(V.tensor_tensor(xn[:, :, :], xc[:, :, :], per_tile(ln_s[:, 4, :], D), ALU.mult), s_ln, at + 7)
                return first, second, third

            def residue(x, s_first, s_done, s_parts, parts, r, bank):
                dve.wait_ge(s_first, x + 1)
                if x is not 0:
                    dve.wait_ge(s_parts, 3 * x)
                V.tensor_tensor(r[:, :], ST[bank][:, :], parts[:, 0, :], ALU.subtract).then_inc(s_done, 1)

            def top_steps(x):
                at = TOP_STEPS * x
                T = [tk[:, n, :, :] for n in range(10)]
                C = [tks[:, n, :] for n in range(8)]

                def st(n, make):
                    def run():
                        if n == 1:
                            dve.wait_ge(s_eg, x + 1)
                        else:
                            dve.wait_ge(s_tk, at + n - 1)
                        if n == TOP_STEPS and x is not 0:
                            dve.wait_ge(s_rwT, x)
                        make().then_inc(s_tk, 1)
                    return run

                tt, ts = V.tensor_tensor, V.tensor_scalar
                gate, eq, cand, hot1, rest, hot2, hot, kept = T[0], T[1], T[2], T[3], T[4], T[5], T[6], T[7]
                makes = [
                    lambda: ts(T[8], eg[:, :, :], 1.0, None, ALU.add),
                    lambda: V.reciprocal(gate, T[8]),
                    lambda: V.reduce_max(C[0], gate, AX),
                    lambda: tt(eq, gate, per_tile(C[0], E), ALU.is_ge),
                    lambda: tt(cand, eq, rank[:, :, :], ALU.mult),
                    lambda: V.reduce_max(C[1], cand, AX),
                    lambda: tt(hot1, cand, per_tile(C[1], E), ALU.is_equal),
                    lambda: V.scalar_tensor_tensor(out=rest, in0=hot1, scalar=-2.0, in1=gate, op0=ALU.mult, op1=ALU.add),
                    lambda: V.reduce_max(C[2], rest, AX),
                    lambda: tt(eq, rest, per_tile(C[2], E), ALU.is_ge),
                    lambda: tt(cand, eq, rank[:, :, :], ALU.mult),
                    lambda: V.reduce_max(C[3], cand, AX),
                    lambda: tt(hot2, cand, per_tile(C[3], E), ALU.is_equal),
                    lambda: tt(hot, hot1, hot2, ALU.add),
                    lambda: tt(kept, hot, gate, ALU.mult),
                    lambda: tt(C[4], C[0], C[2], ALU.add),
                    lambda: ts(C[5], C[4], float(SHARED + TOPK), None, ALU.mult),
                    lambda: V.reciprocal(C[6], C[5]),
                    lambda: tt(rw[:, :, :], kept, per_tile(C[6], E), ALU.mult),
                ]
                return [st(n + 1, m) for n, m in enumerate(makes)]

            def row_max(x, u):
                dve.wait_ge(s_s, UNITS * x + u + 1)
                V.reduce_max(rowmax[:, u // 2, u % 2 * 2:u % 2 * 2 + 2], S[u % 2][:, :, :], AX).then_inc(s_mx, 1)

            def split_max(x):
                at = MS_STEPS * x
                if x is 0:
                    dve.wait_ge(s_pad, 1)
                dve.wait_ge(s_mx, UNITS * (x + 1))
                if x is not 0:
                    dve.wait_ge(s_mT, x)
                m = rowmax[:, :, :].rearrange("p m t -> p t m")
                step(V.tensor_scalar(mparts[:, :, 0, :], m, -1.0, None, ALU.mult), s_ms, at + 1)
                step(V.tensor_tensor(mres[:, :, 0, :], m, mparts[:, :, 0, :], ALU.add), s_ms, at + 2)
                step(V.tensor_scalar(mparts[:, :, 1, :], mres[:, :, 0, :], -1.0, None, ALU.mult), s_ms, at + 3)
                step(V.tensor_tensor(mres[:, :, 1, :], mres[:, :, 0, :], mparts[:, :, 1, :], ALU.add), s_ms, at + 4)
                step(V.tensor_scalar(mparts[:, :, 2, :], mres[:, :, 1, :], -1.0, None, ALU.mult), s_ms, at + 5)

            for part in norm_steps(0):
                part()
            V.memset(kop[0][64:ROWS, :, :], 1.0).then_inc(s_kone, 1)
            dve.wait_ge(s_small, 64)
            step(V.tensor_scalar(omd[:, :], dw_col[:, :], -1.0, 1.0, ALU.mult, ALU.add), s_const, 1)
            step(V.tensor_scalar(ndw[:, :], dw_col[:, :], -1.0, None, ALU.mult), s_const, 2)
            step(V.tensor_tensor(wos[:, :], nw_col[:, :], omd[:, :], ALU.mult), s_const, 3)
            step(V.tensor_tensor(bos[:, :], bo_col[:, :], omd[:, :], ALU.mult), s_const, 4)
            dve.wait_ge(s_wTc, 3)
            V.tensor_scalar(woT[:, :], ST[0][:, 3 * P:4 * P], wos[:, 0:1], None, ALU.mult).then_inc(s_woT, 1)
            residue(0, s_q1, s_qr, s_q3, qparts, qres, 2)
            residue(0, s_k1, s_kr, s_k3, kparts, kres, 0)
            for part in norm_steps(1):
                part()
            V.memset(kop[1][64:ROWS, :, :], 1.0).then_inc(s_kone, 1)
            residue(1, s_q1, s_qr, s_q3, qparts, qres, 2)
            residue(1, s_k1, s_kr, s_k3, kparts, kres, 0)
            for e in range(E):
                last = V.memset(rank[:, :, e:e + 1], float(E - e))
            last.then_inc(s_rank, 1)
            dve.wait_ge(s_rank, 1)
            top = top_steps(0)
            for u in range(UNITS):
                row_max(0, u)
                if u < TOP_STEPS:
                    top[u]()
            split_max(0)

            def residual(b):
                dve.wait_ge(s_u, b + 1)
                dve.wait_ge(s_xr, 16 * b + 16)
                V.tensor_tensor(res[:, :, :].rearrange("p t d -> p (t d)"), O[:, :],
                                res[:, :, :].rearrange("p t d -> p (t d)"), ALU.add).then_inc(s_out, 1)

            def attend(b, par, more, behind):
                if more:
                    top = top_steps(b + 1)
                    for u in range(UNITS):
                        row_max(b + 1, u)
                        if behind and u == 1:
                            residual(b - 1)
                        if 4 <= u < 4 + TOP_STEPS:
                            top[u - 4]()
                elif behind:
                    residual(b - 1)

            def unpack_o(b, t):
                at = OE_STEPS * b + 4 * t
                o = ST[(2, 0, 1, 2)[t]][:, :].rearrange("p (m c) -> p m c", m=HM)
                dve.wait_ge(s_ot, QT * b + t + 1)
                step(V.reciprocal(o_inv[:, :].unsqueeze(2), o[:, :, DH:DH + 1]), s_on, at + 1)
                second = o_inv[:, :].rearrange("p (h i) -> p h i", i=MAPS)[:, :, 1:2]
                step(V.tensor_scalar(second, second, ndw[:, 0:1], None, ALU.mult), s_on, at + 2)
                step(V.tensor_tensor(o_sc[:, :, :], o[:, :, 0:DH], per_tile(o_inv[:, :], DH), ALU.mult), s_on, at + 3)
                both = o_sc[:, :, :].rearrange("p (h i) e -> p h i e", i=MAPS)
                step(V.tensor_tensor(o_n[:, t, :].rearrange("p (h e) -> p h e", h=H), both[:, :, 0, :],
                                     both[:, :, 1, :], ALU.add), s_on, at + 4)

            def rms_norm(b):
                at = OE_STEPS * b + 4 * QT
                step(V.tensor_tensor(sq[:, :, :], o_n[:, :, :], o_n[:, :, :], ALU.mult), s_on, at + 1)
                step(V.reduce_sum(o_st[:, 0, :], sq[:, :, :], AX), s_on, at + 2)
                step(V.tensor_scalar(o_st[:, 1, :], o_st[:, 0, :], 1.0 / D, RMS_EPS, ALU.mult, ALU.add), s_on, at + 3)

            def rms_scale(b):
                dve.wait_ge(s_rp, b + 1)
                step(V.tensor_tensor(o_n[:, :, :], o_n[:, :, :], per_tile(o_st[:, 0, :], D), ALU.mult), s_on,
                     OE_STEPS * (b + 1))

            def ffn(b, par, more, prep):
                parts = norm_steps(b + 2) if prep else None
                for c in range(CH):
                    dve.wait_ge(s_si, CH * b + c + 1)
                    dve.wait_ge(s_h3, CH * b + c + 1)
                    if c >= NHB:
                        dve.wait_ge(s_y, CH * b + c - NHB + 1)
                    V.tensor_tensor(hid[:, c % NHB, :], S[c % 2][:, 1, :], sil[:, c % 2, :], ALU.mult)\
                     .then_inc(s_hm, 1)
                    if more and c == 1:
                        split_max(b + 1)
                    if prep and c in (3, 5, 7):
                        parts[c // 2 - 1]()
                    if c in (2, 4, 6, 8):
                        unpack_o(b, c // 2 - 1)
                    if c == 9:
                        rms_norm(b)
                    if prep and c == 10:
                        residue(b + 2, s_q1, s_qr, s_q3, qparts, qres, 1)
                    if prep and c == 11:
                        residue(b + 2, s_k1, s_kr, s_k3, kparts, kres, 2)
                    if c == 12:
                        rms_scale(b)

            batches(dve, attend, ffn)
            residual(BATCH - 1)

        @block.tensor
        def _(pe):
            mm, tr = nc.tensor.matmul, nc.tensor.transpose

            def tiles_T(dst, src, idn, s):
                for t in range(QT):
                    last = tr(dst[:, t * P:(t + 1) * P], src(t), idn)
                last.then_inc(s, 1)

            def do_xT(x, bank):
                pe.wait_ge(s_ln, LN_STEPS * x + LN_STEPS)
                tiles_T(ST[bank][:, :], lambda t: xn[:, t, :], ident[:, :], s_xT)

            def project(x, j, bank, s):
                pe.wait_ge(s_xTc, x + 1)
                mm(ST[bank][:, :], wqkvT[:, j, :], xT[:, :], start=True, stop=True).then_inc(s, 1)

            def do_v(x, bank):
                for t in range(QT):
                    last = mm(ST[bank][:, t * P:(t + 1) * P], xT[:, t * P:(t + 1) * P], wqkvT[:, 2, :],
                              start=True, stop=True)
                last.then_inc(s_v, 1)

            def do_g(x, bank):
                for t in range(QT):
                    last = mm(ST[bank][:, t * E:(t + 1) * E], xT[:, t * P:(t + 1) * P], wg[:, :],
                              start=True, stop=True)
                last.then_inc(s_g, 1)

            def do_rwT(x, bank=0):
                pe.wait_ge(s_tk, TOP_STEPS * x + TOP_STEPS)
                tiles_T(ST[bank][0:E, :], lambda t: rw[:, t, :], ident[:, :], s_rwT)

            def do_mT(x, bank):
                pe.wait_ge(s_ms, MS_STEPS * x + MS_STEPS)
                tiles_T(ST[bank][:, 0:SEQ // 2].bitcast(bf16), lambda t: mpad[:, t, :], ident_b[:, :], s_mT)

            def score_unit(x, par, u, half):
                if half == 0 and u >= 2:
                    pe.wait_ge(s_mx, UNITS * x + u - 1)
                t = u % 2 * 2 + half
                ins = mm(S[u % 2][:, half, :], qop[par][0:TERMS, u // 2, t * P:(t + 1) * P],
                         kop[par][0:TERMS, u // 2, :], start=True, stop=True)
                if half == 1:
                    ins.then_inc(s_s, 1)

            pe.wait_ge(s_id, 4)
            pe.wait_ge(s_wraw, 64)
            for j in range(4):
                last = tr(ST[0][:, j * P:(j + 1) * P], w_raw[:, j, :], ident[:, :])
            last.then_inc(s_wT, 1)
            do_xT(0, 1)
            pe.wait_ge(s_wTc, 3)
            project(0, 0, 2, s_q)
            pe.wait_ge(s_woT, 1)
            project(0, 1, 0, s_k)
            do_v(0, 1)
            pe.wait_ge(s_small, 64)
            pe.wait_ge(s_qr, 1)
            do_g(0, 2)
            pe.wait_ge(s_vc, 1)
            do_xT(1, 1)
            pe.wait_ge(s_z, 1)
            project(1, 0, 2, s_q)
            pe.wait_ge(s_kr, 1)
            project(1, 1, 0, s_k)
            do_v(1, 1)
            pe.wait_ge(s_qr, 2)
            do_g(1, 2)
            pe.wait_ge(s_ql[0], 48)
            pe.wait_ge(s_kl[0], 48)
            for u in range(UNITS):
                for half in range(2):
                    score_unit(0, 0, u, half)
            pe.wait_ge(s_kr, 2)
            do_mT(0, 0)
            pe.wait_ge(s_vc, 2)
            do_rwT(0, 1)

            def finish(b):
                pe.wait_ge(s_yc, b + 1)
                tiles_T(O[:, :], lambda t: yT[:, t * P:(t + 1) * P], ident[:, :], s_u)

            def attend(b, par, more, behind):
                pe.wait_ge(s_ml, 16 * b + 16)
                pe.wait_ge(s_vc, b + 1)
                if more:
                    pe.wait_ge(s_ql[1 - par], 24 * (b + par) + 48)
                    pe.wait_ge(s_kl[1 - par], 24 * (b + par) + 48)
                for quad in range(GROUPS * QT + 1):
                    if quad < GROUPS * QT:
                        g, t = divmod(quad, QT)
                        for j in range(4):
                            s = 4 * quad + j
                            if s == 0:
                                pe.wait_ge(s_mc, b + 1)
                                pe.wait_ge(s_rwc, b + 1)
                                if more:
                                    pe.wait_ge(s_vc, b + 2)
                                    pe.wait_ge(s_z, b + 2)
                            if s >= 3:
                                pe.wait_ge(s_p, TILES * b + s - 2)
                            m = 4 * g + j
                            mm(ST[s % 3][:, :], kop[par][:, m, t * P:(t + 1) * P], qop[par][:, m, :],
                               start=True, stop=True).then_inc(s_st, 1)
                            if more:
                                score_unit(b + 1, 1 - par, 2 * quad + j // 2, j % 2)
                    if quad == 0 and behind:
                        finish(b - 1)
                    if quad:
                        g, t = divmod(quad - 1, QT)
                        if quad == 1 and behind:
                            pe.wait_ge(s_out, b)
                        if t == 0 and g:
                            pe.wait_ge(s_oe, GROUPS * b + g)
                        for j in range(4):
                            s = 4 * (quad - 1) + j
                            pe.wait_ge(s_p, TILES * b + s + 1)
                            mm(O[VW * j:VW * (j + 1), :], vop[par][:, t, (4 * g + j) // MAPS, :],
                               probs[:, s % NP, :], start=(t == 0), stop=(t == QT - 1),
                               tile_position=(0, VW * j)).then_inc(s_av, 1)

            def do_oT(b, t, bank):
                for g in range(GROUPS):
                    last = tr(ST[bank][:, g * P:(g + 1) * P], oT[:, g, t * P:(t + 1) * P], ident[:, :])
                last.then_inc(s_ot, 1)

            def down(b, c):
                if c < SHARED * FC:
                    pe.wait_ge(s_hm, CH * b + c + 1)
                    h = hid[:, c % NHB, :]
                else:
                    pe.wait_ge(s_hw, RCH * b + c - SHARED * FC + 1)
                    h = hidw[:, c % NHB, :]
                mm(O[:, :], w2[:, c // FC, c % FC, :], h, start=(c == 0), stop=False).then_inc(s_y, 1)

            def ffn(b, par, more, prep):
                pe.wait_ge(s_p, TILES * (b + 1))
                pe.wait_ge(s_oe, GROUPS * (b + 1))
                pe.wait_ge(s_xs, 2 * b + 2)
                if more:
                    pe.wait_ge(s_mx, UNITS * (b + 2))
                pe.wait_ge(s_w13, 2 * (E + SHARED))
                pe.wait_ge(s_w2s, 1)
                for c in range(CH):
                    if c >= 2:
                        pe.wait_ge(s_hm, CH * b + c - 1)
                    for side, s in ((0, s_h1), (1, s_h3)):
                        at = slice(side * FF + c % FC * P, side * FF + c % FC * P + P)
                        dst = S[c % 2][:, side, :]
                        mm(dst, w13h[:, c // FC, at], xh[par][:, :], start=True, stop=False)
                        mm(dst, w13h[:, c // FC, at], xl[par][:, :], start=False, stop=False)
                        mm(dst, w13l[:, c // FC, at], xh[par][:, :], start=False, stop=True).then_inc(s, 1)
                    if c >= LAG:
                        down(b, c - LAG)
                    if more and c == 0:
                        do_rwT(b + 1)
                    if c == 1:
                        do_oT(b, 0, 2)
                    if more and c == 2:
                        do_mT(b + 1, 1)
                    if c == 3:
                        if more:
                            pe.wait_ge(s_rwc, b + 2)
                        do_oT(b, 1, 0)
                    if c == 5:
                        if more:
                            pe.wait_ge(s_mc, b + 2)
                        do_oT(b, 2, 1)
                    if c == 7:
                        pe.wait_ge(s_on, OE_STEPS * b + 4)
                        do_oT(b, 3, 2)
                    if prep:
                        x = b + 2
                        if c == 9:
                            pe.wait_ge(s_on, OE_STEPS * b + 8)
                            do_xT(x, 0)
                        if c == 10:
                            pe.wait_ge(s_on, OE_STEPS * b + 12)
                            project(x, 0, 1, s_q)
                        if c == 11:
                            pe.wait_ge(s_on, OE_STEPS * b + 16)
                            project(x, 1, 2, s_k)
                        if c == 12:
                            do_v(x, 0)
                        if c == 13:
                            pe.wait_ge(s_qr, x + 1)
                            do_g(x, 1)
                    if c == 14:
                        if prep:
                            pe.wait_ge(s_kr, b + 3)
                        pe.wait_ge(s_on, OE_STEPS * (b + 1))
                        tiles_T(ST[2][:, :], lambda t: o_n[:, t, :], ident[:, :], s_nT)
                for c in range(CH - LAG, CH):
                    down(b, c)
                pe.wait_ge(s_nc, b + 1)
                mm(O[:, :], woT[:, :], nT[:, :], start=False, stop=True).then_inc(s_wo, 1)

            batches(pe, attend, ffn)
            finish(BATCH - 1)


_INS = ['L0_attn_x', 'L0_attn_Wq', 'L0_attn_Wk', 'L0_attn_Wv', 'L0_attn_norm_w', 'L0_attn_Wo', 'L0_attn_bo',
        'L0_attn_diff_weight', 'L0_ffn_Wg', 'L0_ffn_Ws1', 'L0_ffn_Ws3', 'L0_ffn_Ws2', 'L0_ffn_We1', 'L0_ffn_We3',
        'L0_ffn_We2']


def kernel(**inputs):
    import numpy as np
    import concourse.bacc as bacc
    from concourse.bass_utils import run_bass_kernel_spmd

    nc = bacc.Bacc("TRN2", target_bir_lowering=False, num_devices=1)
    arrays, args = {}, []
    for name in _INS:
        a = np.ascontiguousarray(inputs[name])
        if a.ndim == 0:
            a = a.reshape(1)
        arrays[f"in_{name}"] = a
        args.append(nc.dram_tensor(f"in_{name}", a.shape, mybir.dt.from_np(a.dtype), kind="ExternalInput").ap())
    shape = inputs['L0_attn_x'].shape
    args.append(nc.dram_tensor("out_x", shape, mybir.dt.float32, kind="ExternalOutput").ap())
    differential_attention_moe_block(nc, *args)
    r = run_bass_kernel_spmd(nc, [arrays], core_ids=[0])
    return r.results[0]["out_x"]
```

```python
import concourse.bass as bass
from concourse import mybir
from contextlib import ExitStack


def differential_attention_moe_block(
    nc: bass.Bass,
    x_in: bass.AP,
    Wq: bass.AP,
    Wk: bass.AP,
    Wv: bass.AP,
    norm_w: bass.AP,
    Wo: bass.AP,
    bo: bass.AP,
    diff_weight: bass.AP,
    Wg: bass.AP,
    Ws1: bass.AP,
    Ws3: bass.AP,
    Ws2: bass.AP,
    We1: bass.AP,
    We3: bass.AP,
    We2: bass.AP,
    out: bass.AP,
):
    f32 = mybir.dt.float32
    f32r = mybir.dt.float32r
    bf16 = mybir.dt.bfloat16
    ALU = mybir.AluOpType
    ACT = mybir.ActivationFunctionType
    AX = mybir.AxisListType.X

    BATCH, SEQ, D = x_in.shape
    H, DH = norm_w.shape
    MAPS = 2
    FD = DH // MAPS
    HM = H * MAPS
    E = We1.shape[0]
    FF = We1.shape[2]
    TOPK, SHARED = 2, 1
    P = 128
    QT = SEQ // P
    PARTS = 3
    TERMS = PARTS * PARTS * FD
    ROWS = TERMS + PARTS
    SCALE = float(FD) ** -0.5
    LN_EPS = 1e-5
    RMS_EPS = 2.0 ** -23
    GROUPS = HM // 4
    TILES = HM * QT
    UNITS = HM * QT // 2
    VW = 32
    NP = 8
    NHB = 4
    FC = FF // P
    CH = (E + SHARED) * FC
    RCH = E * FC
    NRW = 4
    NWB = 2
    LAG = 3
    QK = 16 * PARTS * PARTS
    MD = 16 * PARTS
    FINISH = 4
    EARLY = HM // 2
    LN_STEPS, TOP_STEPS, MS_STEPS, OE_STEPS = 7, 19, 5, 4 * QT + 4

    w_scr = nc.dram_tensor("w_scr", (2, E * SEQ), f32, kind="Internal").ap()

    ctx = ExitStack()
    with ctx:
        def sb(name, shape, dt=f32):
            return ctx.enter_context(nc.sbuf_tensor(name, shape, dt))

        def pb(name, shape):
            return ctx.enter_context(nc.psum_tensor(name, shape, f32))

        def sem(name):
            return ctx.enter_context(nc.semaphore(name))

        ident = sb("ident", [P, P])
        ident_b = sb("ident_b", [P, P], bf16)
        wqkvT = sb("wqkvT", [P, 3, P])
        woT = sb("woT", [P, P])
        nw_col = sb("nw_col", [P, 1])
        bo_col = sb("bo_col", [P, 1])
        dw_col = sb("dw_col", [P, 1])
        ndw = sb("ndw", [P, 1])
        omd = sb("omd", [P, 1])
        wos = sb("wos", [P, 1])
        bos = sb("bos", [P, 1])
        wg = sb("wg", [P, E])
        w13h = sb("w13h", [P, E + SHARED, 2 * FF], f32r)
        w13l = sb("w13l", [P, E + SHARED, 2 * FF], f32r)
        w2h = sb("w2h", [P, E + SHARED, FC, D], f32r)
        w2l = sb("w2l", [P, E + SHARED, FC, D], f32r)
        half = sb("half", [P, QT])
        one = sb("one", [P, 1])
        scrap = sb("scrap", [P, 1])
        rank = sb("rank", [P, QT, E])
        xin = sb("xin", [P, QT, D])
        xc = sb("xc", [P, QT, D])
        sq = sb("sq", [P, QT, D])
        xn = xc
        ln_s = sb("ln_s", [P, 5, QT])
        xT = sb("xT", [P, SEQ])
        xh = [sb(f"xh{i}", [P, SEQ], f32r) for i in range(2)]
        xl = [sb(f"xl{i}", [P, SEQ], f32r) for i in range(2)]
        qparts = sb("qparts", [P, PARTS, SEQ], bf16)
        kparts = sb("kparts", [P, PARTS, SEQ], bf16)
        ones_b = sb("ones_b", [PARTS, SEQ], bf16)
        qop = [sb(f"qop{i}", [ROWS, HM, SEQ], bf16) for i in range(2)]
        kop = [sb(f"kop{i}", [ROWS, HM, SEQ], bf16) for i in range(2)]
        vop = [sb(f"vop{i}", [P, QT, H, VW]) for i in range(2)]
        rowmax = sb("rowmax", [P, HM, QT])
        mpad = sb("mpad", [P, QT, P], bf16)
        mparts = mpad[:, :, 0:PARTS * HM].rearrange("p t (a m) -> p t a m", a=PARTS)
        mres = sb("mres", [P, QT, 2, HM])
        mrows = sb("mrows", [PARTS * HM, SEQ], bf16)
        probs = sb("probs", [P, NP, SEQ])
        oT = sb("oT", [P, GROUPS, SEQ])
        o_inv = sb("o_inv", [P, HM])
        o_sc = sb("o_sc", [P, HM, DH])
        o_n = sb("o_n", [P, QT, D])
        o_st = sb("o_st", [P, 2, QT])
        nT = oT[:, GROUPS - 1, :]
        zg = sb("zg", [P, QT, E])
        eg = sb("eg", [P, QT, E])
        tk = sb("tk", [P, 9, QT, E])
        tks = sb("tks", [P, 8, QT])
        rw = sb("rw", [P, QT, E])
        rwT = sb("rwT", [E, SEQ])
        rwb = sb("rwb", [P, NRW, SEQ])
        sil = sb("sil", [P, 2, SEQ])
        w13 = sil
        hid = probs[:, 0:NHB, :]
        qres = probs[:, NP - 2, :]
        kres = probs[:, NP - 1, :]
        hh = sb("hh", [P, 2, SEQ], f32r)
        hl = sb("hl", [P, 2, SEQ], f32r)
        w2n = (E + SHARED) * FC * D
        w2 = probs[:, 0:-(-w2n // SEQ), :].rearrange("p a s -> p (a s)")[:, 0:w2n]\
            .rearrange("p (e c d) -> p e c d", c=FC, d=D)
        yT = nT
        res = sb("res", [P, QT, D])
        w_raw = res

        S = [pb(f"S{i}", [P, 2, SEQ]) for i in range(2)]
        ST = [pb(f"ST{i}", [P, SEQ]) for i in range(3)]
        O = pb("O", [P, SEQ])

        def tile_bank(s, more):
            banks = [st[:, :] for st in ST] + [S[n][:, half, :] for n in range(2) for half in range(2)]
            return banks[s % banks_for(more)]

        def banks_for(more):
            return 3 if more else 7

        s_wraw, s_small, s_wbig = sem("w_raw_loaded"), sem("small_loaded"), sem("w_big_loaded")
        s_id, s_wT, s_wTc, s_const = sem("ident_set"), sem("wT_ready"), sem("wT_copied"), sem("const_steps")
        s_half, s_pad, s_v0, s_w13, s_kone = sem("half_set"), sem("pad_set"), sem("v_set"), sem("w13_split"), sem("k_ones_set")
        s_w13l = [sem(f"w13_loaded{n}") for n in range(NWB)]
        s_woT, s_w2s = sem("woT_ready"), sem("w2_scaled")
        s_xin, s_ln, s_xT, s_xTc, s_xs = sem("x_loaded"), sem("ln_steps"), sem("xT_ready"), sem("xT_copied"), sem("x_split")
        s_q, s_k, s_v, s_g = sem("q_ready"), sem("k_ready"), sem("v_ready"), sem("g_ready")
        s_q1, s_k1, s_vc, s_z = sem("q1_ready"), sem("k1_ready"), sem("v_copied"), sem("z_copied")
        s_qr, s_kr, s_q3, s_k3 = sem("q_res"), sem("k_res"), sem("q_split"), sem("k_split")
        s_k0, s_ql, s_kl = sem("k0_last_part_loaded"), [sem("q_loaded0"), sem("q_loaded1")], [sem("k_loaded0"), sem("k_loaded1")]
        s_eg, s_tk, s_rwT, s_rwc = sem("gate_exp"), sem("top_steps"), sem("rwT_ready"), sem("rwT_copied")
        s_rws, s_rwb = sem("rw_stored"), [sem(f"rw_loaded{n}") for n in range(NRW)]
        s_s, s_mx, s_ms, s_mT, s_mc = sem("s_ready"), sem("max_ready"), sem("max_split"), sem("mT_ready"), sem("m_copied")
        s_ml = sem("m_loaded")
        s_st, s_p, s_av, s_oe = sem("st_ready"), sem("probs_ready"), sem("av_done"), sem("o_copied")
        s_ot, s_on, s_nT, s_nc = sem("oT_ready"), sem("o_steps"), sem("nT_ready"), sem("nT_copied")
        s_h1, s_h3, s_si, s_hm, s_hw = sem("h1_ready"), sem("h3_ready"), sem("silu_ready"), sem("hid_ready"), sem("hidw_ready")
        s_y, s_yc, s_u = sem("down_done"), sem("y_copied"), sem("u_ready")
        s_rs, s_rp = sem("ln_pow"), sem("rms_pow")
        s_rank, s_warm, s_ones = sem("rank_set"), sem("table_warm"), sem("ones_set")
        s_hh, s_hl = sem("hh_ready"), sem("hl_ready")
        s_xr, s_out, s_ost = sem("xres_loaded"), sem("res_ready"), sem("out_stored")

        block = ctx.enter_context(nc.Block())

        def batches(eng, attend, ffn):
            attend(0, 0, more=True, behind=False)
            with eng.Fori(0, BATCH // 2 - 1) as i:
                for par in range(2):
                    ffn(2 * i + par, par, more=True, prep=True)
                    attend(2 * i + par + 1, 1 - par, more=True, behind=True)
            ffn(BATCH - 2, 0, more=True, prep=False)
            attend(BATCH - 1, 1, more=False, behind=True)
            ffn(BATCH - 1, 1, more=False, prep=False)

        def q_rows(x, par):
            return QK // 2 * (x - par) + QK

        def k_rows(x, par):
            return QK // 2 * (x - par) + QK - (16 * PARTS if par == 0 else 0)

        def lay_part(eng, x, par, a, s_first, s_parts, parts, op, s_rows, step, turn):
            if a == 0:
                eng.wait_ge(s_first, x + 1)
            else:
                eng.wait_ge(s_parts, 3 * x + 2 * a - 1)
            for r in range(PARTS):
                at = (step * a + turn * r) * FD
                eng.dma_start(op[par][at:at + FD, :, :], parts[:, a, :]).then_inc(s_rows[par], 16)

        @block.sync
        def _(sp):
            sp.dma_start(xin[:, :, :], x_in[0].rearrange("(t p) d -> p t d", p=P)).then_inc(s_xin, 16)
            for j, w in enumerate((Wq, Wk, Wv, Wo)):
                sp.dma_start(w_raw[:, j, :], w).then_inc(s_wraw, 16)
            sp.dma_start(nw_col[:, :], norm_w.rearrange("h (e o) -> (h e) o", o=1)).then_inc(s_small, 16)
            sp.dma_start(bo_col[:, :], bo.rearrange("(d o) -> d o", o=1)).then_inc(s_small, 16)
            sp.dma_start(dw_col[:, :], diff_weight.partition_broadcast(P)).then_inc(s_small, 16)
            sp.dma_start(wg[:, :], Wg).then_inc(s_small, 16)
            sp.dma_start(w2[:, 0, :, :], Ws2.rearrange("(c f) d -> f c d", f=P)).then_inc(s_wbig, 16)
            for c in range(FC):
                sp.dma_start(w2[:, 1:, c, :], We2[:, c * P:(c + 1) * P, :].rearrange("e f d -> f e d"))\
                  .then_inc(s_wbig, 16)

            def load_x(x):
                sp.wait_ge(s_ln, LN_STEPS * (x - 1) + 3)
                sp.dma_start(xin[:, :, :], x_in[x].rearrange("(t p) d -> p t d", p=P)).then_inc(s_xin, 16)

            def lay_qk(x, par, k_parts=PARTS):
                for a in range(PARTS):
                    lay_part(sp, x, par, a, s_q1, s_q3, qparts, qop, s_ql, step=PARTS, turn=1)
                for a in range(k_parts):
                    lay_part(sp, x, par, a, s_k1, s_k3, kparts, kop, s_kl, step=1, turn=PARTS)

            def lay_m(n, par, m0=0, m1=HM):
                sp.wait_ge(s_mc, n + 1)
                for a in range(PARTS):
                    sp.dma_start(qop[par][TERMS + a:TERMS + a + 1, m0:m1, :], mrows[a * HM + m0:a * HM + m1, :])\
                      .then_inc(s_ml, 16)

            def store_rw(x, par):
                sp.wait_ge(s_rwc, x + 1)
                sp.dma_start(w_scr[par].rearrange("(e t) -> e t", e=E), rwT[:, :]).then_inc(s_rws, 16)

            def load_rw(x, par):
                sp.wait_ge(s_rws, 16 * x + 16)
                sp.wait_ge(s_hw, RCH * x)
                for e in range(NRW):
                    sp.dma_start(rwb[:, e, :], w_scr[par, e * SEQ:(e + 1) * SEQ].partition_broadcast(P))\
                      .then_inc(s_rwb[e], 16)

            def load_res(b):
                sp.dma_start(res[:, :, :], x_in[b].rearrange("(t p) d -> p t d", p=P)).then_inc(s_xr, 16)

            load_x(1)
            sp.wait_ge(s_ones, 1)
            for i in range(2):
                sp.dma_start(kop[i][TERMS:ROWS, :, :], ones_b[:, :].unsqueeze(1).to_broadcast([PARTS, HM, SEQ]))\
                  .then_inc(s_kone, 16)
            lay_qk(0, 0, k_parts=PARTS - 1)
            lay_qk(1, 1)
            store_rw(0, 0)
            load_rw(0, 0)
            lay_m(0, 0, 0, EARLY)
            lay_m(1, 0, EARLY, HM)
            sp.wait_ge(s_wT, 1)
            load_res(0)

            def store_out(b):
                sp.wait_ge(s_out, b + 1)
                sp.dma_start(out[b].rearrange("(t p) d -> p t d", p=P), res[:, :, :]).then_inc(s_ost, 16)

            def attend(b, par, more, behind):
                if behind:
                    store_out(b - 1)
                    sp.wait_ge(s_ost, 16 * b)
                    load_res(b)

            def ffn(b, par, more, prep):
                if prep:
                    load_x(b + 2)
                if more:
                    store_rw(b + 1, 1 - par)
                    lay_m(b + 2, 1 - par)
                if prep:
                    sp.wait_ge(s_st, TILES * (b + 1))
                    lay_qk(b + 2, par)
                if more:
                    load_rw(b + 1, 1 - par)

            batches(sp, attend, ffn)
            store_out(BATCH - 1)
            sp.wait_ge(s_ost, 16 * BATCH)

        @block.gpsimd
        def _(gp):
            nc.gpsimd.memset(half[:, :], -0.5).then_inc(s_half, 1)
            nc.gpsimd.memset(one[:, :], 1.0).then_inc(s_half, 1)
            nc.gpsimd.memset(ident[:, :], 0.0).then_inc(s_id, 1)
            nc.gpsimd.memset(ident_b[:, :], 0.0).then_inc(s_id, 1)
            gp.wait_ge(s_id, 2)
            for m in (ident, ident_b):
                nc.gpsimd.affine_select(out=m[:, :], in_=m[:, :], compare_op=ALU.not_equal, fill=1.0, base=0,
                                        pattern=[[-1, P]], channel_multiplier=1).then_inc(s_id, 1)

            def split(x, n, s_res, s_parts, parts, r):
                if n == 0:
                    gp.wait_ge(s_res, x + 1)
                    nc.gpsimd.tensor_tensor(parts[:, 1, :], r, ones, ALU.mult).then_inc(s_parts, 1)
                if n == 1:
                    gp.wait_ge(s_parts, 3 * x + 1)
                    nc.gpsimd.tensor_tensor(r, r, parts[:, 1, :], ALU.subtract).then_inc(s_parts, 1)
                if n == 2:
                    gp.wait_ge(s_parts, 3 * x + 2)
                    nc.gpsimd.tensor_tensor(parts[:, 2, :], r, ones, ALU.mult).then_inc(s_parts, 1)

            def split_q(x, n):
                split(x, n, s_qr, s_q3, qparts, qres)

            def split_k(x, n):
                split(x, n, s_kr, s_k3, kparts, kres)

            def split_x(x, par):
                gp.wait_ge(s_xTc, x + 1)
                nc.gpsimd.tensor_tensor(xh[par][:, :], xT[:, :], ones, ALU.mult).then_inc(s_xs, 1)
                gp.wait_ge(s_xs, 2 * x + 1)
                nc.gpsimd.tensor_tensor(xl[par][:, :], xT[:, :], xh[par][:, :].bitcast(f32), ALU.subtract)\
                  .then_inc(s_xs, 1)

            def load_w13(e):
                for side, (ws, we) in enumerate(((Ws1, We1), (Ws3, We3))):
                    gp.dma_start(w13[:, e % NWB, side * FF:(side + 1) * FF], we[e - SHARED] if e else ws)\
                      .then_inc(s_w13l[e % NWB], 16)

            gp.wait_ge(s_half, 2)
            ones = one[:, :].to_broadcast([P, SEQ])

            def norm_pow(x):
                gp.wait_ge(s_ln, LN_STEPS * x + 6)
                nc.gpsimd.tensor_tensor(ln_s[:, 4, :], ln_s[:, 3, :], half[:, :], ALU.pow).then_inc(s_rs, 1)

            def rms_pow(b):
                gp.wait_ge(s_on, OE_STEPS * b + 4 * QT + 3)
                nc.gpsimd.tensor_tensor(o_st[:, 0, :], o_st[:, 1, :], half[:, :], ALU.pow).then_inc(s_rp, 1)

            for i in range(2):
                nc.gpsimd.memset(vop[i][:, :, :, :], 0.0).then_inc(s_v0, 1)
            gp.wait_ge(s_v0, 2)
            for i in range(2):
                nc.gpsimd.memset(vop[i][:, :, :, DH:DH + 1], 1.0).then_inc(s_v0, 1)
            nc.gpsimd.memset(mpad[:, :, :], 0.0).then_inc(s_pad, 1)
            norm_pow(0)
            for n in range(3):
                split_q(0, n)
            lay_part(gp, 0, 0, PARTS - 1, s_k1, s_k3, kparts, kop, [s_k0], step=1, turn=PARTS)
            norm_pow(1)
            for e in range(NWB):
                load_w13(e)
            split_x(0, 0)
            for n in range(3):
                split_q(1, n)
            for n in range(3):
                split_k(1, n)
            split_x(1, 1)
            gp.wait_ge(s_wbig, 16 * (1 + FC))
            nc.gpsimd.tensor_scalar(w2[:, 0, :, :], w2[:, 0, :, :], 1.0 / (SHARED + TOPK), None, ALU.mult)\
              .then_inc(s_w2s, 1)
            gp.wait_ge(s_w2s, 1)
            nc.gpsimd.tensor_copy(w2h[:, :, :, :], w2).then_inc(s_w2s, 1)
            gp.wait_ge(s_w2s, 2)
            nc.gpsimd.tensor_tensor(w2l[:, :, :, :], w2, w2h[:, :, :, :].bitcast(f32), ALU.subtract)\
              .then_inc(s_w2s, 1)
            for e in range(E + SHARED):
                gp.wait_ge(s_w13l[e % NWB], 32 * (e // NWB + 1))
                nc.gpsimd.tensor_copy(w13h[:, e, :], w13[:, e % NWB, :]).then_inc(s_w13, 1)
                gp.wait_ge(s_w13, 2 * e + 1)
                nc.gpsimd.tensor_tensor(w13l[:, e, :], w13[:, e % NWB, :], w13h[:, e, :].bitcast(f32), ALU.subtract)\
                  .then_inc(s_w13, 1)
                if e + NWB < E + SHARED:
                    gp.wait_ge(s_w13, 2 * e + 2)
                    load_w13(e + NWB)

            def attend(b, par, more, behind):
                pass

            def ffn(b, par, more, prep):
                for c in range(CH):
                    if prep and c == 3:
                        norm_pow(b + 2)
                    if c >= SHARED * FC:
                        e = c // FC - SHARED
                        if c % FC == 0:
                            gp.wait_ge(s_rwb[e % NRW], 16 * (E // NRW) * b + 16 * (e // NRW + 1))
                        gp.wait_ge(s_hm, CH * b + c + 1)
                        nc.gpsimd.tensor_tensor(hid[:, c % NHB, :], hid[:, c % NHB, :], rwb[:, e % NRW, :],
                                                ALU.mult).then_inc(s_hw, 1)
                    if c == 13:
                        rms_pow(b)
                    if prep and 8 <= c < 11:
                        split_q(b + 2, c - 8)
                    if prep and 11 <= c < 14:
                        split_k(b + 2, c - 11)
                if prep:
                    gp.wait_ge(s_h3, CH * (b + 1))
                    split_x(b + 2, par)

            batches(gp, attend, ffn)

        @block.scalar
        def _(act):
            def copy_xT(x, first=False):
                act.wait_ge(s_xT, x + 1)
                if not first:
                    act.wait_ge(s_xs, 2 * x)
                    act.wait_ge(s_g, x)
                nc.scalar.activation(xT[:, :], ST[1][:, :], ACT.Copy).then_inc(s_xTc, 1)

            def copy_q(x, par, first=False):
                act.wait_ge(s_q, x + 1)
                if not first:
                    act.wait_ge(s_ql[1 - par], q_rows(x - 1, 1 - par))
                nc.scalar.activation(qparts[:, 0, :], ST[2][:, :], ACT.Copy).then_inc(s_q1, 1)

            def copy_k(x, par, first=False, second=False):
                act.wait_ge(s_k, x + 1)
                if not first:
                    act.wait_ge(s_kl[1 - par], k_rows(x - 1, 1 - par))
                if second:
                    act.wait_ge(s_k0, 16 * PARTS)
                nc.scalar.activation(kparts[:, 0, :], ST[0][:, :], ACT.Copy).then_inc(s_k1, 1)

            def copy_v(x, par):
                act.wait_ge(s_v, x + 1)
                nc.scalar.activation(vop[par][:, :, :, 0:DH],
                                     ST[1][:, :].rearrange("p (t h e) -> p t h e", t=QT, h=H),
                                     ACT.Copy).then_inc(s_vc, 1)

            def copy_z(x, bank):
                act.wait_ge(s_g, x + 1)
                nc.scalar.activation(zg[:, :, :].rearrange("p t e -> p (t e)"), ST[bank][:, 0:QT * E], ACT.Copy)\
                   .then_inc(s_z, 1)

            def gate_exp(x):
                act.wait_ge(s_z, x + 1)
                act.wait_ge(s_tk, TOP_STEPS * x)
                nc.scalar.activation(eg[:, :, :], zg[:, :, :], ACT.Exp, scale=-1.0).then_inc(s_eg, 1)

            def copy_rwT(x, bank=0):
                act.wait_ge(s_rwT, x + 1)
                act.wait_ge(s_rws, 16 * x)
                nc.scalar.activation(rwT[:, :], ST[bank][0:E, :], ACT.Copy).then_inc(s_rwc, 1)

            def copy_m(n, bank, first=False):
                act.wait_ge(s_mT, n + 1)
                if not first:
                    act.wait_ge(s_ml, MD * n)
                nc.scalar.activation(mrows[:, :], bank[0:PARTS * HM, 0:SEQ // 2].bitcast(bf16), ACT.Copy)\
                   .then_inc(s_mc, 1)

            act.wait_ge(s_wT, 1)
            for j in range(2):
                nc.scalar.activation(wqkvT[:, j, :].rearrange("p (f m) -> p m f", m=HM),
                                     ST[0][:, j * P:(j + 1) * P].rearrange("p (m f) -> p m f", m=HM),
                                     ACT.Copy).then_inc(s_wTc, 1)
            nc.scalar.activation(wqkvT[:, 2, :], ST[0][:, 2 * P:3 * P], ACT.Copy).then_inc(s_wTc, 1)
            copy_xT(0, first=True)
            copy_q(0, 0, first=True)
            copy_k(0, 0, first=True)
            act.wait_ge(s_v0, 4)
            copy_v(0, 0)
            copy_z(0, 2)
            gate_exp(0)
            copy_xT(1)
            copy_q(1, 1)
            copy_k(1, 1, second=True)
            copy_v(1, 1)
            copy_z(1, 2)
            copy_rwT(0, 1)
            copy_m(0, ST[0], first=True)

            def warm(func):
                nc.scalar.activation(scrap[:, :], bos[:, 0:1], func).then_inc(s_warm, 1)

            def attend(b, par, more, behind):
                if not behind:
                    act.wait_ge(s_w2s, 3)
                for s in range(TILES):
                    if behind and s < 2:
                        act.wait_ge(s_hl, CH * b - 1 + s)
                    act.wait_ge(s_st, TILES * b + s + 1)
                    if s >= NP:
                        act.wait_ge(s_av, TILES * b + s - NP + 1)
                    nc.scalar.activation(probs[:, s % NP, :], tile_bank(s, more), ACT.Exp, scale=SCALE).then_inc(s_p, 1)
                    if more and s == 2:
                        gate_exp(b + 1)
                    if behind and s == 1:
                        copy_y(b - 1)
                    if not behind and s == 3:
                        copy_m(1, O)
                    if more and s % 16 == 4 and s > 16:
                        copy_o(b, s // 16 - 1)
                warm(ACT.Silu)
                if more:
                    copy_o(b, GROUPS - 1)

            def copy_y(b):
                act.wait_ge(s_y, CH * (b + 1))
                nc.scalar.activation(yT[:, :], O[:, :], ACT.Identity, bias=bos[:, 0:1]).then_inc(s_yc, 1)

            def copy_o(b, g):
                act.wait_ge(s_av, TILES * b + 16 * (g + 1))
                nc.scalar.activation(oT[:, g, :], O[:, :], ACT.Copy).then_inc(s_oe, 1)

            def round_hid(b, c):
                if c < SHARED * FC:
                    act.wait_ge(s_hm, CH * b + c + 1)
                else:
                    act.wait_ge(s_hw, RCH * b + c - SHARED * FC + 1)
                if c >= 2:
                    act.wait_ge(s_y, CH * b + c - 1)
                nc.scalar.activation(hh[:, c % 2, :], hid[:, c % NHB, :], ACT.Copy).then_inc(s_hh, 1)

            def load_rw(b, par, e):
                act.wait_ge(s_hw, RCH * b + (e - NRW + 1) * FC)
                act.dma_start(rwb[:, e % NRW, :], w_scr[par, e * SEQ:(e + 1) * SEQ].partition_broadcast(P))\
                   .then_inc(s_rwb[e % NRW], 16)

            def ffn(b, par, more, prep):
                for c in range(CH):
                    if c >= 2:
                        round_hid(b, c - 2)
                    act.wait_ge(s_h1, CH * b + c + 1)
                    if c >= 2:
                        act.wait_ge(s_hm, CH * b + c - 1)
                    nc.scalar.activation(sil[:, c % 2, :], S[c % 2][:, 0, :], ACT.Silu).then_inc(s_si, 1)
                    e = c // 2 - SHARED + 2
                    if c % 2 == 0 and NRW <= e < E:
                        load_rw(b, par, e)
                    if more and c == 0:
                        copy_rwT(b + 1)
                    if more and c == 2:
                        copy_m(b + 2, ST[1])
                    if prep:
                        if c == 5:
                            copy_xT(b + 2)
                        if c == 6:
                            copy_q(b + 2, par)
                        if c == 7:
                            copy_k(b + 2, par)
                        if c == 9:
                            copy_v(b + 2, par)
                        if c == 11:
                            copy_z(b + 2, 1)
                    if c == 16:
                        act.wait_ge(s_nT, b + 1)
                        nc.scalar.activation(nT[:, :], ST[2][:, :], ACT.Copy).then_inc(s_nc, 1)
                round_hid(b, CH - 2)
                round_hid(b, CH - 1)
                if more:
                    warm(ACT.Exp)
                else:
                    copy_y(b)

            batches(act, attend, ffn)

        @block.vector
        def _(dve):
            V = nc.vector

            def step(ins, s, n):
                ins.then_inc(s, 1)
                dve.wait_ge(s, n)

            def per_tile(col, width):
                return col.unsqueeze(2).to_broadcast([P, col.shape[1], width])

            def chained(makes, s, at, waits):
                def link(n, make):
                    def run():
                        if n:
                            dve.wait_ge(s, at + n)
                        if n in waits:
                            waits[n]()
                        make().then_inc(s, 1)
                    return run
                return [link(n, make) for n, make in enumerate(makes)]

            def norm_steps(x, first=False):
                def loaded():
                    dve.wait_ge(s_xin, 16 * x + 16)

                def free():
                    if not first:
                        dve.wait_ge(s_xT, x)

                def rooted():
                    dve.wait_ge(s_rs, x + 1)
                return chained([
                    lambda: V.reduce_sum(ln_s[:, 0, :], xin[:, :, :], AX),
                    lambda: V.tensor_scalar(ln_s[:, 1, :], ln_s[:, 0, :], -1.0 / D, None, ALU.mult),
                    lambda: V.tensor_tensor(xc[:, :, :], xin[:, :, :], per_tile(ln_s[:, 1, :], D), ALU.add),
                    lambda: V.tensor_tensor(sq[:, :, :], xc[:, :, :], xc[:, :, :], ALU.mult),
                    lambda: V.reduce_sum(ln_s[:, 2, :], sq[:, :, :], AX),
                    lambda: V.tensor_scalar(ln_s[:, 3, :], ln_s[:, 2, :], 1.0 / D, LN_EPS, ALU.mult, ALU.add),
                    lambda: V.tensor_tensor(xn[:, :, :], xc[:, :, :], per_tile(ln_s[:, 4, :], D), ALU.mult),
                ], s_ln, LN_STEPS * x, {0: loaded, 2: free, 6: rooted})

            def residue(x, s_first, s_done, s_parts, parts, r, bank):
                dve.wait_ge(s_first, x + 1)
                if x is not 0:
                    dve.wait_ge(s_parts, 3 * x)
                V.tensor_tensor(r, ST[bank][:, :], parts[:, 0, :], ALU.subtract).then_inc(s_done, 1)

            def top_steps(x):
                at = TOP_STEPS * x
                T = [tk[:, n, :, :] for n in range(9)]
                C = [tks[:, n, :] for n in range(8)]

                def st(n, make):
                    def run():
                        if n == 1:
                            dve.wait_ge(s_eg, x + 1)
                        else:
                            dve.wait_ge(s_tk, at + n - 1)
                        if n == TOP_STEPS and x is not 0:
                            dve.wait_ge(s_rwT, x)
                        make().then_inc(s_tk, 1)
                    return run

                tt, ts = V.tensor_tensor, V.tensor_scalar
                gate, eq, cand, hot1, rest, hot2, hot, kept = T[0], T[1], T[2], T[3], T[4], T[5], T[6], T[7]
                makes = [
                    lambda: ts(T[8], eg[:, :, :], 1.0, None, ALU.add),
                    lambda: V.reciprocal(gate, T[8]),
                    lambda: V.reduce_max(C[0], gate, AX),
                    lambda: tt(eq, gate, per_tile(C[0], E), ALU.is_ge),
                    lambda: tt(cand, eq, rank[:, :, :], ALU.mult),
                    lambda: V.reduce_max(C[1], cand, AX),
                    lambda: tt(hot1, cand, per_tile(C[1], E), ALU.is_equal),
                    lambda: V.scalar_tensor_tensor(out=rest, in0=hot1, scalar=-2.0, in1=gate, op0=ALU.mult, op1=ALU.add),
                    lambda: V.reduce_max(C[2], rest, AX),
                    lambda: tt(eq, rest, per_tile(C[2], E), ALU.is_ge),
                    lambda: tt(cand, eq, rank[:, :, :], ALU.mult),
                    lambda: V.reduce_max(C[3], cand, AX),
                    lambda: tt(hot2, cand, per_tile(C[3], E), ALU.is_equal),
                    lambda: tt(hot, hot1, hot2, ALU.add),
                    lambda: tt(kept, hot, gate, ALU.mult),
                    lambda: tt(C[4], C[0], C[2], ALU.add),
                    lambda: ts(C[5], C[4], float(SHARED + TOPK), None, ALU.mult),
                    lambda: V.reciprocal(C[6], C[5]),
                    lambda: tt(rw[:, :, :], kept, per_tile(C[6], E), ALU.mult),
                ]
                return [st(n + 1, m) for n, m in enumerate(makes)]

            def row_max(x, u):
                dve.wait_ge(s_s, UNITS * x + u + 1)
                V.reduce_max(rowmax[:, u // 2, u % 2 * 2:u % 2 * 2 + 2], S[u % 2][:, :, :], AX).then_inc(s_mx, 1)

            def split_max(n, x, m0=0, m1=HM, first=False):
                def reduced():
                    if first:
                        dve.wait_ge(s_pad, 1)
                    else:
                        dve.wait_ge(s_mT, n)
                    dve.wait_ge(s_mx, UNITS * x + 2 * m1)
                m = rowmax[:, m0:m1, :].rearrange("p m t -> p t m")
                part = [mparts[:, :, a, m0:m1] for a in range(PARTS)]
                left = [mres[:, :, a, m0:m1] for a in range(PARTS - 1)]
                return chained([
                    lambda: V.tensor_scalar(part[0], m, -1.0, None, ALU.mult),
                    lambda: V.tensor_tensor(left[0], m, part[0], ALU.add),
                    lambda: V.tensor_scalar(part[1], left[0], -1.0, None, ALU.mult),
                    lambda: V.tensor_tensor(left[1], left[0], part[1], ALU.add),
                    lambda: V.tensor_scalar(part[2], left[1], -1.0, None, ALU.mult),
                ], s_ms, MS_STEPS * n, {0: reduced})

            V.memset(ones_b[:, :], 1.0).then_inc(s_ones, 1)
            for run in norm_steps(0, first=True):
                run()
            dve.wait_ge(s_small, 64)
            step(V.tensor_scalar(omd[:, :], dw_col[:, :], -1.0, 1.0, ALU.mult, ALU.add), s_const, 1)
            step(V.tensor_scalar(ndw[:, :], dw_col[:, :], -1.0, None, ALU.mult), s_const, 2)
            step(V.tensor_tensor(wos[:, :], nw_col[:, :], omd[:, :], ALU.mult), s_const, 3)
            step(V.tensor_tensor(bos[:, :], bo_col[:, :], omd[:, :], ALU.mult), s_const, 4)
            dve.wait_ge(s_wTc, 3)
            V.tensor_scalar(woT[:, :], ST[0][:, 3 * P:4 * P], wos[:, 0:1], None, ALU.mult).then_inc(s_woT, 1)
            norm1 = norm_steps(1)
            for run in norm1[:3]:
                run()
            residue(0, s_q1, s_qr, s_q3, qparts, qres, 2)
            residue(0, s_k1, s_kr, s_k3, kparts, kres, 0)
            for n, part in ((1, 1), (3, 2)):
                dve.wait_ge(s_kr if n == 1 else s_k3, 1 if n == 1 else 2)
                V.tensor_copy(kparts[:, part, :], kres).then_inc(s_k3, 1)
                if n == 1:
                    dve.wait_ge(s_k3, 1)
                    V.tensor_tensor(kres, kres, kparts[:, 1, :], ALU.subtract).then_inc(s_k3, 1)
            for run in norm1[3:]:
                run()
            for e in range(E):
                last = V.memset(rank[:, :, e:e + 1], float(E - e))
            last.then_inc(s_rank, 1)
            dve.wait_ge(s_rank, 1)
            top = top_steps(0)
            early = split_max(0, 0, 0, EARLY, first=True)
            for u in range(UNITS):
                row_max(0, u)
                if u < TOP_STEPS:
                    top[u]()
                if u == 5:
                    residue(1, s_q1, s_qr, s_q3, qparts, qres, 2)
                if u == 7:
                    residue(1, s_k1, s_kr, s_k3, kparts, kres, 0)
                if 0 <= u - 2 * EARLY - 2 < MS_STEPS:
                    early[u - 2 * EARLY - 2]()
            for run in split_max(1, 0, EARLY, HM):
                run()

            def residual(b):
                dve.wait_ge(s_u, b + 1)
                dve.wait_ge(s_xr, 16 * b + 16)
                V.tensor_tensor(res[:, :, :].rearrange("p t d -> p (t d)"), O[:, :],
                                res[:, :, :].rearrange("p t d -> p (t d)"), ALU.add).then_inc(s_out, 1)

            def attend(b, par, more, behind):
                if more:
                    top = top_steps(b + 1)
                    for u in range(UNITS):
                        row_max(b + 1, u)
                        if behind and u == 1:
                            residual(b - 1)
                        if 4 <= u < 4 + TOP_STEPS:
                            top[u - 4]()
                else:
                    residual(b - 1)
                    for g in range(GROUPS):
                        dve.wait_ge(s_av, TILES * b + 16 * (g + 1))
                        V.tensor_copy(oT[:, g, :], O[:, :]).then_inc(s_oe, 1)

            def unpack_o(b, t):
                o = ST[(2, 0)[t % 2]][:, :].rearrange("p (m c) -> p m c", m=HM)
                second = o_inv[:, :].rearrange("p (h i) -> p h i", i=MAPS)[:, :, 1:2]
                both = o_sc[:, :, :].rearrange("p (h i) e -> p h i e", i=MAPS)
                return [
                    lambda: V.reciprocal(o_inv[:, :].unsqueeze(2), o[:, :, DH:DH + 1]),
                    lambda: V.tensor_scalar(second, second, ndw[:, 0:1], None, ALU.mult),
                    lambda: V.tensor_tensor(o_sc[:, :, :], o[:, :, 0:DH], per_tile(o_inv[:, :], DH), ALU.mult),
                    lambda: V.tensor_tensor(o_n[:, t, :].rearrange("p (h e) -> p h e", h=H), both[:, :, 0, :],
                                            both[:, :, 1, :], ALU.add),
                ]

            def o_steps(b):
                def transposed(t):
                    return lambda: dve.wait_ge(s_ot, QT * b + t + 1)

                def rooted():
                    dve.wait_ge(s_rp, b + 1)
                waits = {4 * t: transposed(t) for t in range(QT)}
                waits[4 * QT + 3] = rooted
                return chained([make for t in range(QT) for make in unpack_o(b, t)] + [
                    lambda: V.tensor_tensor(sq[:, :, :], o_n[:, :, :], o_n[:, :, :], ALU.mult),
                    lambda: V.reduce_sum(o_st[:, 0, :], sq[:, :, :], AX),
                    lambda: V.tensor_scalar(o_st[:, 1, :], o_st[:, 0, :], 1.0 / D, RMS_EPS, ALU.mult, ALU.add),
                    lambda: V.tensor_tensor(o_n[:, :, :], o_n[:, :, :], per_tile(o_st[:, 0, :], D), ALU.mult),
                ], s_on, OE_STEPS * b, waits)

            SIDE = {0: [("n", 0), ("n", 1)], 1: [("n", 2), ("n", 3)],
                    2: [("o", 0), ("n", 4), ("o", 1), ("n", 5)], 3: [("o", 2), ("o", 3)],
                    4: [("n", 6), ("o", 4), ("o", 5)], 5: [("o", 6), ("o", 7)],
                    9: [("o", 8), ("o", 9)], 10: [("o", 10), ("o", 11)],
                    11: [("o", 12), ("o", 13), ("o", 14)], 12: [("o", 15), ("o", 16), ("o", 17)],
                    13: [("o", 18)], 14: [("o", 19)]}

            def rest_hid(b, c):
                dve.wait_ge(s_hh, CH * b + c + 1)
                if c >= 2:
                    dve.wait_ge(s_y, CH * b + c - 1)
                V.tensor_tensor(hl[:, c % 2, :], hid[:, c % NHB, :], hh[:, c % 2, :].bitcast(f32), ALU.subtract)\
                 .then_inc(s_hl, 1)

            def ffn(b, par, more, prep):
                norm = norm_steps(b + 2) if prep else None
                o = o_steps(b)
                if more:
                    for run in split_max(b + 2, b + 1):
                        run()
                for c in range(CH):
                    if c >= 2:
                        rest_hid(b, c - 2)
                    dve.wait_ge(s_si, CH * b + c + 1)
                    dve.wait_ge(s_h3, CH * b + c + 1)
                    V.tensor_tensor(hid[:, c % NHB, :], S[c % 2][:, 1, :], sil[:, c % 2, :], ALU.mult)\
                     .then_inc(s_hm, 1)
                    for chain, n in SIDE.get(c, ()):
                        if chain == "o":
                            o[n]()
                        elif prep:
                            norm[n]()
                    if prep and c == 7:
                        residue(b + 2, s_q1, s_qr, s_q3, qparts, qres, 2)
                    if prep and c == 8:
                        residue(b + 2, s_k1, s_kr, s_k3, kparts, kres, 0)
                rest_hid(b, CH - 2)
                rest_hid(b, CH - 1)

            batches(dve, attend, ffn)
            residual(BATCH - 1)

        @block.tensor
        def _(pe):
            mm, tr = nc.tensor.matmul, nc.tensor.transpose

            def tiles_T(dst, src, idn, s):
                for t in range(QT):
                    last = tr(dst[:, t * P:(t + 1) * P], src(t), idn)
                last.then_inc(s, 1)

            def do_xT(x, bank):
                pe.wait_ge(s_ln, LN_STEPS * x + LN_STEPS)
                tiles_T(ST[bank][:, :], lambda t: xn[:, t, :], ident[:, :], s_xT)

            def project(x, j, bank, s):
                pe.wait_ge(s_xTc, x + 1)
                mm(ST[bank][:, :], wqkvT[:, j, :], xT[:, :], start=True, stop=True).then_inc(s, 1)

            def do_v(x, bank):
                for t in range(QT):
                    last = mm(ST[bank][:, t * P:(t + 1) * P], xT[:, t * P:(t + 1) * P], wqkvT[:, 2, :],
                              start=True, stop=True)
                last.then_inc(s_v, 1)

            def do_g(x, bank):
                for t in range(QT):
                    last = mm(ST[bank][:, t * E:(t + 1) * E], xT[:, t * P:(t + 1) * P], wg[:, :],
                              start=True, stop=True)
                last.then_inc(s_g, 1)

            def do_rwT(x, bank=0):
                pe.wait_ge(s_tk, TOP_STEPS * x + TOP_STEPS)
                tiles_T(ST[bank][0:E, :], lambda t: rw[:, t, :], ident[:, :], s_rwT)

            def do_mT(n, bank):
                pe.wait_ge(s_ms, MS_STEPS * n + MS_STEPS)
                tiles_T(bank[:, 0:SEQ // 2].bitcast(bf16), lambda t: mpad[:, t, :], ident_b[:, :], s_mT)

            def score_unit(x, par, u, half, first=False):
                if half == 0 and (u >= 2 or not first):
                    pe.wait_ge(s_mx, UNITS * x + u - 1)
                t = u % 2 * 2 + half
                ins = mm(S[u % 2][:, half, :], qop[par][0:TERMS, u // 2, t * P:(t + 1) * P],
                         kop[par][0:TERMS, u // 2, :], start=True, stop=True)
                if half == 1:
                    ins.then_inc(s_s, 1)

            def keep_busy(n):
                for _ in range(n):
                    mm(O[:, 0:P], ident_b[:, :], ident_b[:, :], start=True, stop=True)

            pe.wait_ge(s_id, 4)
            keep_busy(28)
            pe.wait_ge(s_wraw, 64)
            for j in range(4):
                last = tr(ST[0][:, j * P:(j + 1) * P], w_raw[:, j, :], ident[:, :])
            last.then_inc(s_wT, 1)
            keep_busy(40)
            do_xT(0, 1)
            pe.wait_ge(s_wTc, 3)
            project(0, 0, 2, s_q)
            pe.wait_ge(s_woT, 1)
            project(0, 1, 0, s_k)
            do_v(0, 1)
            pe.wait_ge(s_small, 64)
            pe.wait_ge(s_qr, 1)
            do_g(0, 2)
            keep_busy(130)
            pe.wait_ge(s_ql[0], q_rows(0, 0))
            pe.wait_ge(s_kl[0], k_rows(0, 0))
            pe.wait_ge(s_k0, 16 * PARTS)
            for u in range(UNITS):
                for half in range(2):
                    score_unit(0, 0, u, half, first=True)
                if u == 1:
                    pe.wait_ge(s_vc, 1)
                    do_xT(1, 1)
                if u == 3:
                    pe.wait_ge(s_z, 1)
                    project(1, 0, 2, s_q)
                if u == 5:
                    pe.wait_ge(s_kr, 1)
                    project(1, 1, 0, s_k)
                if u == 7:
                    do_v(1, 1)
                if u == 9:
                    pe.wait_ge(s_qr, 2)
                    do_g(1, 2)
                if u == TOP_STEPS + 2:
                    pe.wait_ge(s_vc, 2)
                    do_rwT(0, 1)
                if u == 2 * EARLY + MS_STEPS + 3:
                    pe.wait_ge(s_kr, 2)
                    do_mT(0, ST[0])

            def finish(b):
                pe.wait_ge(s_yc, b + 1)
                tiles_T(O[:, :], lambda t: yT[:, t * P:(t + 1) * P], ident[:, :], s_u)

            def score_tile(b, par, s, more):
                if s == 0:
                    pe.wait_ge(s_rwc, b + 1)
                if s == 0 and more:
                    pe.wait_ge(s_vc, b + 2)
                    pe.wait_ge(s_z, b + 2)
                if s >= banks_for(more):
                    pe.wait_ge(s_p, TILES * b + s + 1 - banks_for(more))
                m, t = s // (4 * QT) * 4 + s % 4, s // 4 % QT
                mm(tile_bank(s, more), kop[par][:, m, t * P:(t + 1) * P], qop[par][:, m, :],
                   start=True, stop=True).then_inc(s_st, 1)
                if more:
                    score_unit(b + 1, 1 - par, s // 2, s % 2)

            def start_attend(b, par, more, behind, s):
                if s == 0:
                    pe.wait_ge(s_kone, 32)
                    pe.wait_ge(s_ml, MD * b + (2 * MD if behind else MD))
                    if more:
                        pe.wait_ge(s_ql[1 - par], q_rows(b + 1, 1 - par))
                        pe.wait_ge(s_kl[1 - par], k_rows(b + 1, 1 - par))
                score_tile(b, par, s, more)

            def attend(b, par, more, behind):
                pe.wait_ge(s_vc, b + 1)
                if not behind:
                    for s in range(3):
                        start_attend(b, par, more, behind, s)
                for quad in range(GROUPS * QT + 1):
                    if quad < GROUPS * QT:
                        for s in range(4 * quad, 4 * quad + 4):
                            if not behind and s == EARLY * QT:
                                pe.wait_ge(s_ml, 2 * MD)
                            if s >= 3:
                                score_tile(b, par, s, more)
                            if s == FINISH and behind:
                                finish(b - 1)
                    if quad == 0 and not behind:
                        do_mT(1, O)
                    if quad:
                        g, t = divmod(quad - 1, QT)
                        if quad == 1 and behind:
                            pe.wait_ge(s_out, b)
                        if quad == 1 and not behind:
                            pe.wait_ge(s_mc, 2)
                        if t == 0 and g:
                            pe.wait_ge(s_oe, GROUPS * b + g)
                        for j in range(4):
                            s = 4 * (quad - 1) + j
                            pe.wait_ge(s_p, TILES * b + s + 1)
                            mm(O[VW * j:VW * (j + 1), :], vop[par][:, t, (4 * g + j) // MAPS, :],
                               probs[:, s % NP, :], start=(t == 0), stop=(t == QT - 1),
                               tile_position=(0, VW * j)).then_inc(s_av, 1)

            def do_oT(b, t, bank):
                for g in range(GROUPS):
                    last = tr(ST[bank][:, g * P:(g + 1) * P], oT[:, g, t * P:(t + 1) * P], ident[:, :])
                last.then_inc(s_ot, 1)

            def down(b, c, last=False):
                pe.wait_ge(s_hl, CH * b + c + 1)
                wh, wl = w2h[:, c // FC, c % FC, :], w2l[:, c // FC, c % FC, :]
                mm(O[:, :], wh, hh[:, c % 2, :], start=(c == 0), stop=False)
                mm(O[:, :], wh, hl[:, c % 2, :], start=False, stop=False)
                mm(O[:, :], wl, hh[:, c % 2, :], start=False, stop=last).then_inc(s_y, 1)

            def ffn(b, par, more, prep):
                pe.wait_ge(s_p, TILES * (b + 1))
                pe.wait_ge(s_xs, 2 * b + 2)
                pe.wait_ge(s_w13, 2 * (E + SHARED))
                pe.wait_ge(s_w2s, 3)
                for c in range(CH):
                    if more and c < 2:
                        pe.wait_ge(s_mx, UNITS * (b + 2) - 1 + c)
                    if c >= 2:
                        pe.wait_ge(s_hm, CH * b + c - 1)
                    for side, s in ((0, s_h1), (1, s_h3)):
                        at = slice(side * FF + c % FC * P, side * FF + c % FC * P + P)
                        dst = S[c % 2][:, side, :]
                        mm(dst, w13h[:, c // FC, at], xh[par][:, :], start=True, stop=False)
                        mm(dst, w13h[:, c // FC, at], xl[par][:, :], start=False, stop=False)
                        mm(dst, w13l[:, c // FC, at], xh[par][:, :], start=False, stop=True).then_inc(s, 1)
                    if c >= LAG:
                        down(b, c - LAG)
                    if more and c == 0:
                        do_rwT(b + 1)
                    if c == 1:
                        pe.wait_ge(s_oe, GROUPS * (b + 1))
                        do_oT(b, 0, 2)
                    if more and c == 2:
                        do_mT(b + 2, ST[1])
                    if c == 3:
                        if more:
                            pe.wait_ge(s_rwc, b + 2)
                        do_oT(b, 1, 0)
                    if prep:
                        x = b + 2
                        if c == 5:
                            pe.wait_ge(s_mc, b + 3)
                            do_xT(x, 1)
                        if c == 6:
                            pe.wait_ge(s_on, OE_STEPS * b + 4)
                            project(x, 0, 2, s_q)
                        if c == 7:
                            pe.wait_ge(s_on, OE_STEPS * b + 8)
                            project(x, 1, 0, s_k)
                        if c == 9:
                            do_v(x, 1)
                        if c == 11:
                            pe.wait_ge(s_vc, x + 1)
                            do_g(x, 1)
                    if c == 8:
                        pe.wait_ge(s_on, OE_STEPS * b + 4)
                        if prep:
                            pe.wait_ge(s_qr, b + 3)
                        do_oT(b, 2, 2)
                    if c == 10:
                        pe.wait_ge(s_on, OE_STEPS * b + 8)
                        if prep:
                            pe.wait_ge(s_kr, b + 3)
                        do_oT(b, 3, 0)
                    if c == 16:
                        pe.wait_ge(s_on, OE_STEPS * (b + 1))
                        tiles_T(ST[2][:, :], lambda t: o_n[:, t, :], ident[:, :], s_nT)
                for c in range(CH - LAG, CH):
                    if more:
                        s = c - CH + LAG
                        if s < 2 and prep:
                            pe.wait_ge(s_hm, CH * (b + 1) - 1)
                        if s == 2:
                            pe.wait_ge(s_nc, b + 1)
                            pe.wait_ge(s_hm, CH * (b + 1))
                        start_attend(b + 1, 1 - par, prep, True, s)
                    if c == CH - 1:
                        pe.wait_ge(s_nc, b + 1)
                        mm(O[:, :], woT[:, :], nT[:, :], start=False, stop=False)
                    down(b, c, last=c == CH - 1)

            batches(pe, attend, ffn)
            finish(BATCH - 1)


_INS = ['L0_attn_x', 'L0_attn_Wq', 'L0_attn_Wk', 'L0_attn_Wv', 'L0_attn_norm_w', 'L0_attn_Wo', 'L0_attn_bo',
        'L0_attn_diff_weight', 'L0_ffn_Wg', 'L0_ffn_Ws1', 'L0_ffn_Ws3', 'L0_ffn_Ws2', 'L0_ffn_We1', 'L0_ffn_We3',
        'L0_ffn_We2']


def kernel(**inputs):
    import numpy as np
    import concourse.bacc as bacc
    from concourse.bass_utils import run_bass_kernel_spmd

    nc = bacc.Bacc("TRN2", target_bir_lowering=False, num_devices=1)
    arrays, args = {}, []
    for name in _INS:
        a = np.ascontiguousarray(inputs[name])
        if a.ndim == 0:
            a = a.reshape(1)
        arrays[f"in_{name}"] = a
        args.append(nc.dram_tensor(f"in_{name}", a.shape, mybir.dt.from_np(a.dtype), kind="ExternalInput").ap())
    shape = inputs['L0_attn_x'].shape
    args.append(nc.dram_tensor("out_x", shape, mybir.dt.float32, kind="ExternalOutput").ap())
    differential_attention_moe_block(nc, *args)
    r = run_bass_kernel_spmd(nc, [arrays], core_ids=[0])
    return r.results[0]["out_x"]
```

```python
import concourse.bass as bass
from concourse import mybir
from contextlib import ExitStack


def differential_attention_moe_block(
    nc: bass.Bass,
    x_in: bass.AP,
    Wq: bass.AP,
    Wk: bass.AP,
    Wv: bass.AP,
    norm_w: bass.AP,
    Wo: bass.AP,
    bo: bass.AP,
    diff_weight: bass.AP,
    Wg: bass.AP,
    Ws1: bass.AP,
    Ws3: bass.AP,
    Ws2: bass.AP,
    We1: bass.AP,
    We3: bass.AP,
    We2: bass.AP,
    out: bass.AP,
):
    f32 = mybir.dt.float32
    f32r = mybir.dt.float32r
    bf16 = mybir.dt.bfloat16
    ALU = mybir.AluOpType
    ACT = mybir.ActivationFunctionType
    AX = mybir.AxisListType.X

    BATCH, SEQ, D = x_in.shape
    H, DH = norm_w.shape
    MAPS = 2
    FD = DH // MAPS
    HM = H * MAPS
    E = We1.shape[0]
    FF = We1.shape[2]
    TOPK, SHARED = 2, 1
    P = 128
    QT = SEQ // P
    PARTS = 3
    TERMS = PARTS * PARTS * FD
    ROWS = TERMS + PARTS
    SCALE = float(FD) ** -0.5
    LN_EPS = 1e-5
    RMS_EPS = 2.0 ** -23
    GROUPS = HM // 4
    TILES = HM * QT
    UNITS = HM * QT // 2
    VW = 32
    NP = 8
    NHB = 4
    FC = FF // P
    CH = (E + SHARED) * FC
    RCH = E * FC
    NRW = 4
    NWB = 2
    LAG = 3
    QK = 16 * PARTS * PARTS
    MD = 16 * PARTS
    FINISH = 4
    EARLY = HM // 2
    EARLY_UNIT = 2 * EARLY + 2
    BUSY_ID, BUSY_W = 28, 40
    LN_STEPS, TOP_STEPS, MS_STEPS, OE_STEPS = 7, 19, 5, 4 * QT + 4

    w_scr = nc.dram_tensor("w_scr", (2, E * SEQ), f32, kind="Internal").ap()

    ctx = ExitStack()
    with ctx:
        def sb(name, shape, dt=f32):
            return ctx.enter_context(nc.sbuf_tensor(name, shape, dt))

        def pb(name, shape):
            return ctx.enter_context(nc.psum_tensor(name, shape, f32))

        def sem(name):
            return ctx.enter_context(nc.semaphore(name))

        ident = sb("ident", [P, P])
        ident_b = sb("ident_b", [P, P], bf16)
        wqkvT = sb("wqkvT", [P, 3, P])
        woT = sb("woT", [P, P])
        nw_col = sb("nw_col", [P, 1])
        bo_col = sb("bo_col", [P, 1])
        dw_col = sb("dw_col", [P, 1])
        ndw = sb("ndw", [P, 1])
        omd = sb("omd", [P, 1])
        wos = sb("wos", [P, 1])
        bos = sb("bos", [P, 1])
        wg = sb("wg", [P, E])
        w13h = sb("w13h", [P, E + SHARED, 2 * FF], f32r)
        w13l = sb("w13l", [P, E + SHARED, 2 * FF], f32r)
        w2h = sb("w2h", [P, E + SHARED, FC, D], f32r)
        w2l = sb("w2l", [P, E + SHARED, FC, D], f32r)
        half = sb("half", [P, QT])
        one = sb("one", [P, 1])
        scrap = sb("scrap", [P, 1])
        rank = sb("rank", [P, QT, E])
        xin = sb("xin", [P, QT, D])
        xc = sb("xc", [P, QT, D])
        sq = sb("sq", [P, QT, D])
        xn = xc
        ln_s = sb("ln_s", [P, 5, QT])
        xT = sb("xT", [P, SEQ])
        xh = [sb(f"xh{i}", [P, SEQ], f32r) for i in range(2)]
        xl = [sb(f"xl{i}", [P, SEQ], f32r) for i in range(2)]
        qparts = sb("qparts", [P, PARTS, SEQ], bf16)
        kparts = sb("kparts", [P, PARTS, SEQ], bf16)
        ones_b = sb("ones_b", [PARTS, SEQ], bf16)
        qop = [sb(f"qop{i}", [ROWS, HM, SEQ], bf16) for i in range(2)]
        kop = [sb(f"kop{i}", [ROWS, HM, SEQ], bf16) for i in range(2)]
        vop = [sb(f"vop{i}", [P, QT, H, VW]) for i in range(2)]
        rowmax = sb("rowmax", [P, HM, QT])
        mpad = sb("mpad", [P, QT, P], bf16)
        mparts = mpad[:, :, 0:PARTS * HM].rearrange("p t (a m) -> p t a m", a=PARTS)
        mres = sb("mres", [P, QT, 2, HM])
        mrows = sb("mrows", [PARTS * HM, SEQ], bf16)
        probs = sb("probs", [P, NP, SEQ])
        oT = sb("oT", [P, GROUPS, SEQ])
        o_inv = sb("o_inv", [P, HM])
        o_sc = sb("o_sc", [P, HM, DH])
        o_n = sb("o_n", [P, QT, D])
        o_st = sb("o_st", [P, 2, QT])
        nT = oT[:, GROUPS - 1, :]
        zg = sb("zg", [P, QT, E])
        eg = sb("eg", [P, QT, E])
        tk = sb("tk", [P, 9, QT, E])
        tks = sb("tks", [P, 8, QT])
        rw = sb("rw", [P, QT, E])
        rwT = sb("rwT", [E, SEQ])
        rwb = sb("rwb", [P, NRW, SEQ])
        sil = sb("sil", [P, 2, SEQ])
        w13 = sil
        hid = probs[:, 0:NHB, :]
        qres = probs[:, NP - 2, :]
        kres = probs[:, NP - 1, :]
        hh = sb("hh", [P, 2, SEQ], f32r)
        hl = sb("hl", [P, 2, SEQ], f32r)
        w2n = (E + SHARED) * FC * D
        w2 = probs[:, 0:-(-w2n // SEQ), :].rearrange("p a s -> p (a s)")[:, 0:w2n]\
            .rearrange("p (e c d) -> p e c d", c=FC, d=D)
        yT = nT
        res = sb("res", [P, QT, D])
        w_raw = res

        S = [pb(f"S{i}", [P, 2, SEQ]) for i in range(2)]
        ST = [pb(f"ST{i}", [P, SEQ]) for i in range(3)]
        O = pb("O", [P, SEQ])

        def score_banks(more):
            return [st[:, :] for st in ST] + ([] if more else [S[n][:, i, :] for n in range(2) for i in range(2)])

        s_wraw, s_small, s_wbig = sem("w_raw_loaded"), sem("small_loaded"), sem("w_big_loaded")
        s_id, s_wT, s_wTc, s_const = sem("ident_set"), sem("wT_ready"), sem("wT_copied"), sem("const_steps")
        s_half, s_pad, s_v0, s_w13, s_kone = sem("half_set"), sem("pad_set"), sem("v_set"), sem("w13_split"), sem("k_ones_set")
        s_w13l = [sem(f"w13_loaded{n}") for n in range(NWB)]
        s_woT, s_w2s = sem("woT_ready"), sem("w2_scaled")
        s_xin, s_ln, s_xT, s_xTc, s_xs = sem("x_loaded"), sem("ln_steps"), sem("xT_ready"), sem("xT_copied"), sem("x_split")
        s_q, s_k, s_v, s_g = sem("q_ready"), sem("k_ready"), sem("v_ready"), sem("g_ready")
        s_q1, s_k1, s_vc, s_z = sem("q1_ready"), sem("k1_ready"), sem("v_copied"), sem("z_copied")
        s_qr, s_kr, s_q3, s_k3 = sem("q_res"), sem("k_res"), sem("q_split"), sem("k_split")
        s_k0, s_ql, s_kl = sem("k0_last_part_loaded"), [sem("q_loaded0"), sem("q_loaded1")], [sem("k_loaded0"), sem("k_loaded1")]
        s_eg, s_tk, s_rwT, s_rwc = sem("gate_exp"), sem("top_steps"), sem("rwT_ready"), sem("rwT_copied")
        s_rws, s_rwb = sem("rw_stored"), [sem(f"rw_loaded{n}") for n in range(NRW)]
        s_s, s_mx, s_ms, s_mT, s_mc = sem("s_ready"), sem("max_ready"), sem("max_split"), sem("mT_ready"), sem("m_copied")
        s_ml = sem("m_loaded")
        s_st, s_p, s_av, s_oe = sem("st_ready"), sem("probs_ready"), sem("av_done"), sem("o_copied")
        s_ot, s_on, s_nT, s_nc = sem("oT_ready"), sem("o_steps"), sem("nT_ready"), sem("nT_copied")
        s_h1, s_h3, s_si, s_hm, s_hw = sem("h1_ready"), sem("h3_ready"), sem("silu_ready"), sem("hid_ready"), sem("hidw_ready")
        s_y, s_yc, s_u = sem("down_done"), sem("y_copied"), sem("u_ready")
        s_rs, s_rp = sem("ln_pow"), sem("rms_pow")
        s_rank, s_warm, s_ones = sem("rank_set"), sem("table_warm"), sem("ones_set")
        s_hh, s_hl = sem("hh_ready"), sem("hl_ready")
        s_xr, s_out, s_ost = sem("xres_loaded"), sem("res_ready"), sem("out_stored")

        block = ctx.enter_context(nc.Block())

        def batches(eng, attend, ffn):
            attend(0, 0, more=True, behind=False)
            with eng.Fori(0, BATCH // 2 - 1) as i:
                for par in range(2):
                    ffn(2 * i + par, par, more=True, prep=True)
                    attend(2 * i + par + 1, 1 - par, more=True, behind=True)
            ffn(BATCH - 2, 0, more=True, prep=False)
            attend(BATCH - 1, 1, more=False, behind=True)
            ffn(BATCH - 1, 1, more=False, prep=False)

        def q_rows(x, par):
            return QK // 2 * (x - par) + QK

        def k_rows(x, par):
            return QK // 2 * (x - par) + QK - (16 * PARTS if par == 0 else 0)

        def lay_part(eng, x, par, a, s_first, s_parts, parts, op, s_rows, step, turn):
            if a == 0:
                eng.wait_ge(s_first, x + 1)
            else:
                eng.wait_ge(s_parts, 3 * x + 2 * a - 1)
            for r in range(PARTS):
                at = (step * a + turn * r) * FD
                eng.dma_start(op[par][at:at + FD, :, :], parts[:, a, :]).then_inc(s_rows[par], 16)

        @block.sync
        def _(sp):
            sp.dma_start(xin[:, :, :], x_in[0].rearrange("(t p) d -> p t d", p=P)).then_inc(s_xin, 16)
            for j, w in enumerate((Wq, Wk, Wv, Wo)):
                sp.dma_start(w_raw[:, j, :], w).then_inc(s_wraw, 16)
            sp.dma_start(nw_col[:, :], norm_w.rearrange("h (e o) -> (h e) o", o=1)).then_inc(s_small, 16)
            sp.dma_start(bo_col[:, :], bo.rearrange("(d o) -> d o", o=1)).then_inc(s_small, 16)
            sp.dma_start(dw_col[:, :], diff_weight.partition_broadcast(P)).then_inc(s_small, 16)
            sp.dma_start(wg[:, :], Wg).then_inc(s_small, 16)
            sp.dma_start(w2[:, E, :, :], Ws2.rearrange("(c f) d -> f c d", f=P)).then_inc(s_wbig, 16)
            for c in range(FC):
                sp.dma_start(w2[:, 0:E, c, :], We2[:, c * P:(c + 1) * P, :].rearrange("e f d -> f e d"))\
                  .then_inc(s_wbig, 16)

            def load_x(x):
                sp.wait_ge(s_ln, LN_STEPS * (x - 1) + 3)
                sp.dma_start(xin[:, :, :], x_in[x].rearrange("(t p) d -> p t d", p=P)).then_inc(s_xin, 16)

            def lay_qk(x, par, k_parts=PARTS):
                for a in range(PARTS):
                    lay_part(sp, x, par, a, s_q1, s_q3, qparts, qop, s_ql, step=PARTS, turn=1)
                for a in range(k_parts):
                    lay_part(sp, x, par, a, s_k1, s_k3, kparts, kop, s_kl, step=1, turn=PARTS)

            def lay_m(n, par, m0=0, m1=HM):
                sp.wait_ge(s_mc, n + 1)
                for a in range(PARTS):
                    sp.dma_start(qop[par][TERMS + a:TERMS + a + 1, m0:m1, :], mrows[a * HM + m0:a * HM + m1, :])\
                      .then_inc(s_ml, 16)

            def store_rw(x, par):
                sp.wait_ge(s_rwc, x + 1)
                sp.dma_start(w_scr[par].rearrange("(e t) -> e t", e=E), rwT[:, :]).then_inc(s_rws, 16)

            def load_rw(x, par):
                sp.wait_ge(s_rws, 16 * x + 16)
                sp.wait_ge(s_hw, RCH * x)
                for e in range(NRW):
                    sp.dma_start(rwb[:, e, :], w_scr[par, e * SEQ:(e + 1) * SEQ].partition_broadcast(P))\
                      .then_inc(s_rwb[e], 16)

            def load_res(b):
                sp.dma_start(res[:, :, :], x_in[b].rearrange("(t p) d -> p t d", p=P)).then_inc(s_xr, 16)

            load_x(1)
            sp.wait_ge(s_ones, 1)
            for i in range(2):
                sp.dma_start(kop[i][TERMS:ROWS, :, :], ones_b[:, :].unsqueeze(1).to_broadcast([PARTS, HM, SEQ]))\
                  .then_inc(s_kone, 16)
            lay_qk(0, 0, k_parts=PARTS - 1)
            lay_qk(1, 1)
            store_rw(0, 0)
            load_rw(0, 0)
            lay_m(0, 0, 0, EARLY)
            lay_m(1, 0, EARLY, HM)
            sp.wait_ge(s_wT, 1)
            load_res(0)

            def store_out(b):
                sp.wait_ge(s_out, b + 1)
                sp.dma_start(out[b].rearrange("(t p) d -> p t d", p=P), res[:, :, :]).then_inc(s_ost, 16)

            def attend(b, par, more, behind):
                if behind:
                    store_out(b - 1)
                    sp.wait_ge(s_ost, 16 * b)
                    load_res(b)

            def ffn(b, par, more, prep):
                if prep:
                    load_x(b + 2)
                if more:
                    store_rw(b + 1, 1 - par)
                    lay_m(b + 2, 1 - par)
                if prep:
                    sp.wait_ge(s_st, TILES * (b + 1))
                    lay_qk(b + 2, par)
                if more:
                    load_rw(b + 1, 1 - par)

            batches(sp, attend, ffn)
            store_out(BATCH - 1)
            sp.wait_ge(s_ost, 16 * BATCH)

        @block.gpsimd
        def _(gp):
            nc.gpsimd.memset(half[:, :], -0.5).then_inc(s_half, 1)
            nc.gpsimd.memset(one[:, :], 1.0).then_inc(s_half, 1)
            nc.gpsimd.memset(ident[:, :], 0.0).then_inc(s_id, 1)
            nc.gpsimd.memset(ident_b[:, :], 0.0).then_inc(s_id, 1)
            gp.wait_ge(s_id, 2)
            for m in (ident, ident_b):
                nc.gpsimd.affine_select(out=m[:, :], in_=m[:, :], compare_op=ALU.not_equal, fill=1.0, base=0,
                                        pattern=[[-1, P]], channel_multiplier=1).then_inc(s_id, 1)

            def split(x, n, s_res, s_parts, parts, r):
                if n == 0:
                    gp.wait_ge(s_res, x + 1)
                    nc.gpsimd.tensor_tensor(parts[:, 1, :], r, ones, ALU.mult).then_inc(s_parts, 1)
                if n == 1:
                    gp.wait_ge(s_parts, 3 * x + 1)
                    nc.gpsimd.tensor_tensor(r, r, parts[:, 1, :], ALU.subtract).then_inc(s_parts, 1)
                if n == 2:
                    gp.wait_ge(s_parts, 3 * x + 2)
                    nc.gpsimd.tensor_tensor(parts[:, 2, :], r, ones, ALU.mult).then_inc(s_parts, 1)

            def split_q(x, n):
                split(x, n, s_qr, s_q3, qparts, qres)

            def split_k(x, n):
                split(x, n, s_kr, s_k3, kparts, kres)

            def split_x(x, par):
                gp.wait_ge(s_xTc, x + 1)
                nc.gpsimd.tensor_tensor(xh[par][:, :], xT[:, :], ones, ALU.mult).then_inc(s_xs, 1)
                gp.wait_ge(s_xs, 2 * x + 1)
                nc.gpsimd.tensor_tensor(xl[par][:, :], xT[:, :], xh[par][:, :].bitcast(f32), ALU.subtract)\
                  .then_inc(s_xs, 1)

            def load_w13(e):
                for side, (ws, we) in enumerate(((Ws1, We1), (Ws3, We3))):
                    gp.dma_start(w13[:, e % NWB, side * FF:(side + 1) * FF], we[e] if e < E else ws)\
                      .then_inc(s_w13l[e % NWB], 16)

            gp.wait_ge(s_half, 2)
            ones = one[:, :].to_broadcast([P, SEQ])

            def norm_pow(x):
                gp.wait_ge(s_ln, LN_STEPS * x + 6)
                nc.gpsimd.tensor_tensor(ln_s[:, 4, :], ln_s[:, 3, :], half[:, :], ALU.pow).then_inc(s_rs, 1)

            def rms_pow(b):
                gp.wait_ge(s_on, OE_STEPS * b + 4 * QT + 3)
                nc.gpsimd.tensor_tensor(o_st[:, 0, :], o_st[:, 1, :], half[:, :], ALU.pow).then_inc(s_rp, 1)

            for i in range(2):
                nc.gpsimd.memset(vop[i][:, :, :, :], 0.0).then_inc(s_v0, 1)
            gp.wait_ge(s_v0, 2)
            for i in range(2):
                nc.gpsimd.memset(vop[i][:, :, :, DH:DH + 1], 1.0).then_inc(s_v0, 1)
            nc.gpsimd.memset(mpad[:, :, :], 0.0).then_inc(s_pad, 1)
            norm_pow(0)
            for n in range(3):
                split_q(0, n)
            lay_part(gp, 0, 0, PARTS - 1, s_k1, s_k3, kparts, kop, [s_k0], step=1, turn=PARTS)
            norm_pow(1)
            for e in range(NWB):
                load_w13(e)
            split_x(0, 0)
            for n in range(3):
                split_q(1, n)
            for n in range(3):
                split_k(1, n)
            split_x(1, 1)
            gp.wait_ge(s_wbig, 16 * (1 + FC))
            nc.gpsimd.tensor_scalar(w2[:, E, :, :], w2[:, E, :, :], 1.0 / (SHARED + TOPK), None, ALU.mult)\
              .then_inc(s_w2s, 1)
            gp.wait_ge(s_w2s, 1)
            nc.gpsimd.tensor_copy(w2h[:, :, :, :], w2).then_inc(s_w2s, 1)
            gp.wait_ge(s_w2s, 2)
            nc.gpsimd.tensor_tensor(w2l[:, :, :, :], w2, w2h[:, :, :, :].bitcast(f32), ALU.subtract)\
              .then_inc(s_w2s, 1)
            for e in range(E + SHARED):
                gp.wait_ge(s_w13l[e % NWB], 32 * (e // NWB + 1))
                nc.gpsimd.tensor_copy(w13h[:, e, :], w13[:, e % NWB, :]).then_inc(s_w13, 1)
                gp.wait_ge(s_w13, 2 * e + 1)
                nc.gpsimd.tensor_tensor(w13l[:, e, :], w13[:, e % NWB, :], w13h[:, e, :].bitcast(f32), ALU.subtract)\
                  .then_inc(s_w13, 1)
                if e + NWB < E + SHARED:
                    gp.wait_ge(s_w13, 2 * e + 2)
                    load_w13(e + NWB)

            def attend(b, par, more, behind):
                pass

            def ffn(b, par, more, prep):
                for c in range(CH):
                    if prep and c == 3:
                        norm_pow(b + 2)
                    if c < RCH:
                        e = c // FC
                        if c % FC == 0:
                            gp.wait_ge(s_rwb[e % NRW], 16 * (E // NRW) * b + 16 * (e // NRW + 1))
                        gp.wait_ge(s_hm, CH * b + c + 1)
                        nc.gpsimd.tensor_tensor(hid[:, c % NHB, :], hid[:, c % NHB, :], rwb[:, e % NRW, :],
                                                ALU.mult).then_inc(s_hw, 1)
                    if c == 13:
                        rms_pow(b)
                    if prep and 8 <= c < 11:
                        split_q(b + 2, c - 8)
                    if prep and 11 <= c < 14:
                        split_k(b + 2, c - 11)
                if prep:
                    gp.wait_ge(s_h3, CH * (b + 1))
                    split_x(b + 2, par)

            batches(gp, attend, ffn)

        @block.scalar
        def _(act):
            def copy_xT(x, first=False):
                act.wait_ge(s_xT, x + 1)
                if not first:
                    act.wait_ge(s_xs, 2 * x)
                    act.wait_ge(s_g, x)
                nc.scalar.activation(xT[:, :], ST[1][:, :], ACT.Copy).then_inc(s_xTc, 1)

            def copy_q(x, par, first=False):
                act.wait_ge(s_q, x + 1)
                if not first:
                    act.wait_ge(s_ql[1 - par], q_rows(x - 1, 1 - par))
                nc.scalar.activation(qparts[:, 0, :], ST[2][:, :], ACT.Copy).then_inc(s_q1, 1)

            def copy_k(x, par, first=False, second=False):
                act.wait_ge(s_k, x + 1)
                if not first:
                    act.wait_ge(s_kl[1 - par], k_rows(x - 1, 1 - par))
                if second:
                    act.wait_ge(s_k0, 16 * PARTS)
                nc.scalar.activation(kparts[:, 0, :], ST[0][:, :], ACT.Copy).then_inc(s_k1, 1)

            def copy_v(x, par):
                act.wait_ge(s_v, x + 1)
                nc.scalar.activation(vop[par][:, :, :, 0:DH],
                                     ST[1][:, :].rearrange("p (t h e) -> p t h e", t=QT, h=H),
                                     ACT.Copy).then_inc(s_vc, 1)

            def copy_z(x, bank):
                act.wait_ge(s_g, x + 1)
                nc.scalar.activation(zg[:, :, :].rearrange("p t e -> p (t e)"), ST[bank][:, 0:QT * E], ACT.Copy)\
                   .then_inc(s_z, 1)

            def gate_exp(x):
                act.wait_ge(s_z, x + 1)
                act.wait_ge(s_tk, TOP_STEPS * x)
                nc.scalar.activation(eg[:, :, :], zg[:, :, :], ACT.Exp, scale=-1.0).then_inc(s_eg, 1)

            def copy_rwT(x, bank=0):
                act.wait_ge(s_rwT, x + 1)
                act.wait_ge(s_rws, 16 * x)
                nc.scalar.activation(rwT[:, :], ST[bank][0:E, :], ACT.Copy).then_inc(s_rwc, 1)

            def copy_m(n, bank, first=False):
                act.wait_ge(s_mT, n + 1)
                if not first:
                    act.wait_ge(s_ml, MD * n)
                nc.scalar.activation(mrows[:, :], bank[0:PARTS * HM, 0:SEQ // 2].bitcast(bf16), ACT.Copy)\
                   .then_inc(s_mc, 1)

            act.wait_ge(s_wT, 1)
            for j in range(2):
                nc.scalar.activation(wqkvT[:, j, :].rearrange("p (f m) -> p m f", m=HM),
                                     ST[0][:, j * P:(j + 1) * P].rearrange("p (m f) -> p m f", m=HM),
                                     ACT.Copy).then_inc(s_wTc, 1)
            nc.scalar.activation(wqkvT[:, 2, :], ST[0][:, 2 * P:3 * P], ACT.Copy).then_inc(s_wTc, 1)
            copy_xT(0, first=True)
            copy_q(0, 0, first=True)
            copy_k(0, 0, first=True)
            act.wait_ge(s_v0, 4)
            copy_v(0, 0)
            copy_z(0, 2)
            gate_exp(0)
            copy_xT(1)
            copy_q(1, 1)
            copy_k(1, 1, second=True)
            copy_v(1, 1)
            copy_z(1, 2)
            copy_rwT(0, 1)
            copy_m(0, ST[0], first=True)

            def warm(func):
                nc.scalar.activation(scrap[:, :], bos[:, 0:1], func).then_inc(s_warm, 1)

            def attend(b, par, more, behind):
                banks = score_banks(more)
                if not behind:
                    act.wait_ge(s_w2s, 3)
                for s in range(TILES):
                    if behind and s < 2:
                        act.wait_ge(s_hl, CH * b - 1 + s)
                    act.wait_ge(s_st, TILES * b + s + 1)
                    if s >= NP:
                        act.wait_ge(s_av, TILES * b + s - NP + 1)
                    nc.scalar.activation(probs[:, s % NP, :], banks[s % len(banks)], ACT.Exp, scale=SCALE).then_inc(s_p, 1)
                    if more and s == 6:
                        gate_exp(b + 1)
                    if behind and s == 1:
                        copy_y(b - 1)
                    if not behind and s == 3:
                        copy_m(1, O)
                    if more and s % 16 == 4 and s > 16:
                        copy_o(b, s // 16 - 1)
                warm(ACT.Silu)
                if more:
                    copy_o(b, GROUPS - 1)

            def copy_y(b):
                act.wait_ge(s_y, CH * (b + 1))
                nc.scalar.activation(yT[:, :], O[:, :], ACT.Identity, bias=bos[:, 0:1]).then_inc(s_yc, 1)

            def copy_o(b, g):
                act.wait_ge(s_av, TILES * b + 16 * (g + 1))
                nc.scalar.activation(oT[:, g, :], O[:, :], ACT.Copy).then_inc(s_oe, 1)

            def round_hid(b, c):
                if c >= RCH:
                    act.wait_ge(s_hm, CH * b + c + 1)
                else:
                    act.wait_ge(s_hw, RCH * b + c + 1)
                if c >= 2:
                    act.wait_ge(s_y, CH * b + c - 1)
                nc.scalar.activation(hh[:, c % 2, :], hid[:, c % NHB, :], ACT.Copy).then_inc(s_hh, 1)

            def load_rw(b, par, e):
                act.wait_ge(s_hw, RCH * b + (e - NRW + 1) * FC)
                act.dma_start(rwb[:, e % NRW, :], w_scr[par, e * SEQ:(e + 1) * SEQ].partition_broadcast(P))\
                   .then_inc(s_rwb[e % NRW], 16)

            def ffn(b, par, more, prep):
                for c in range(CH):
                    if c >= 2:
                        round_hid(b, c - 2)
                    act.wait_ge(s_h1, CH * b + c + 1)
                    if c >= 2:
                        act.wait_ge(s_hm, CH * b + c - 1)
                    nc.scalar.activation(sil[:, c % 2, :], S[c % 2][:, 0, :], ACT.Silu).then_inc(s_si, 1)
                    e = c // FC + 2
                    if c % 2 == 0 and NRW <= e < E:
                        load_rw(b, par, e)
                    if more and c == 0:
                        copy_rwT(b + 1)
                    if more and c == 2:
                        copy_m(b + 2, ST[1])
                    if prep:
                        if c == 5:
                            copy_xT(b + 2)
                        if c == 6:
                            copy_q(b + 2, par)
                        if c == 7:
                            copy_k(b + 2, par)
                        if c == 9:
                            copy_v(b + 2, par)
                        if c == 11:
                            copy_z(b + 2, 1)
                    if c == 16:
                        act.wait_ge(s_nT, b + 1)
                        nc.scalar.activation(nT[:, :], ST[2][:, :], ACT.Copy).then_inc(s_nc, 1)
                round_hid(b, CH - 2)
                round_hid(b, CH - 1)
                if more:
                    warm(ACT.Exp)
                else:
                    copy_y(b)

            batches(act, attend, ffn)

        @block.vector
        def _(dve):
            V = nc.vector

            def per_tile(col, width):
                return col.unsqueeze(2).to_broadcast([P, col.shape[1], width])

            def norm_step(x, n, first=False):
                if n == 0:
                    dve.wait_ge(s_xin, 16 * x + 16)
                    V.reduce_sum(ln_s[:, 0, :], xin[:, :, :], AX).then_inc(s_ln, 1)
                if n == 1:
                    dve.wait_ge(s_ln, LN_STEPS * x + 1)
                    V.tensor_scalar(ln_s[:, 1, :], ln_s[:, 0, :], -1.0 / D, None, ALU.mult).then_inc(s_ln, 1)
                if n == 2:
                    dve.wait_ge(s_ln, LN_STEPS * x + 2)
                    if not first:
                        dve.wait_ge(s_xT, x)
                    V.tensor_tensor(xc[:, :, :], xin[:, :, :], per_tile(ln_s[:, 1, :], D), ALU.add).then_inc(s_ln, 1)
                if n == 3:
                    dve.wait_ge(s_ln, LN_STEPS * x + 3)
                    V.tensor_tensor(sq[:, :, :], xc[:, :, :], xc[:, :, :], ALU.mult).then_inc(s_ln, 1)
                if n == 4:
                    dve.wait_ge(s_ln, LN_STEPS * x + 4)
                    V.reduce_sum(ln_s[:, 2, :], sq[:, :, :], AX).then_inc(s_ln, 1)
                if n == 5:
                    dve.wait_ge(s_ln, LN_STEPS * x + 5)
                    V.tensor_scalar(ln_s[:, 3, :], ln_s[:, 2, :], 1.0 / D, LN_EPS, ALU.mult, ALU.add).then_inc(s_ln, 1)
                if n == 6:
                    dve.wait_ge(s_ln, LN_STEPS * x + 6)
                    dve.wait_ge(s_rs, x + 1)
                    V.tensor_tensor(xn[:, :, :], xc[:, :, :], per_tile(ln_s[:, 4, :], D), ALU.mult).then_inc(s_ln, 1)

            def residue(x, s_first, s_done, s_parts, parts, r, bank, first=False):
                dve.wait_ge(s_first, x + 1)
                if not first:
                    dve.wait_ge(s_parts, 3 * x)
                V.tensor_tensor(r, ST[bank][:, :], parts[:, 0, :], ALU.subtract).then_inc(s_done, 1)

            def top_step(x, n, first=False):
                gate, eq, cand, hot1, rest, hot2, hot, kept, denom = [tk[:, j, :, :] for j in range(9)]
                max1, rank1, max2, rank2, total, scaled, inv = [tks[:, j, :] for j in range(7)]
                if n == 0:
                    dve.wait_ge(s_eg, x + 1)
                    V.tensor_scalar(denom, eg[:, :, :], 1.0, None, ALU.add).then_inc(s_tk, 1)
                    return
                dve.wait_ge(s_tk, TOP_STEPS * x + n)
                if n == 1:
                    V.reciprocal(gate, denom).then_inc(s_tk, 1)
                if n == 2:
                    V.reduce_max(max1, gate, AX).then_inc(s_tk, 1)
                if n == 3:
                    V.tensor_tensor(eq, gate, per_tile(max1, E), ALU.is_ge).then_inc(s_tk, 1)
                if n == 4:
                    V.tensor_tensor(cand, eq, rank[:, :, :], ALU.mult).then_inc(s_tk, 1)
                if n == 5:
                    V.reduce_max(rank1, cand, AX).then_inc(s_tk, 1)
                if n == 6:
                    V.tensor_tensor(hot1, cand, per_tile(rank1, E), ALU.is_equal).then_inc(s_tk, 1)
                if n == 7:
                    V.scalar_tensor_tensor(out=rest, in0=hot1, scalar=-2.0, in1=gate, op0=ALU.mult, op1=ALU.add)\
                     .then_inc(s_tk, 1)
                if n == 8:
                    V.reduce_max(max2, rest, AX).then_inc(s_tk, 1)
                if n == 9:
                    V.tensor_tensor(eq, rest, per_tile(max2, E), ALU.is_ge).then_inc(s_tk, 1)
                if n == 10:
                    V.tensor_tensor(cand, eq, rank[:, :, :], ALU.mult).then_inc(s_tk, 1)
                if n == 11:
                    V.reduce_max(rank2, cand, AX).then_inc(s_tk, 1)
                if n == 12:
                    V.tensor_tensor(hot2, cand, per_tile(rank2, E), ALU.is_equal).then_inc(s_tk, 1)
                if n == 13:
                    V.tensor_tensor(hot, hot1, hot2, ALU.add).then_inc(s_tk, 1)
                if n == 14:
                    V.tensor_tensor(kept, hot, gate, ALU.mult).then_inc(s_tk, 1)
                if n == 15:
                    V.tensor_tensor(total, max1, max2, ALU.add).then_inc(s_tk, 1)
                if n == 16:
                    V.tensor_scalar(scaled, total, float(SHARED + TOPK), None, ALU.mult).then_inc(s_tk, 1)
                if n == 17:
                    V.reciprocal(inv, scaled).then_inc(s_tk, 1)
                if n == 18:
                    if not first:
                        dve.wait_ge(s_rwT, x)
                    V.tensor_tensor(rw[:, :, :], kept, per_tile(inv, E), ALU.mult).then_inc(s_tk, 1)

            def row_max(x, u):
                dve.wait_ge(s_s, UNITS * x + u + 1)
                V.reduce_max(rowmax[:, u // 2, u % 2 * 2:u % 2 * 2 + 2], S[u % 2][:, :, :], AX).then_inc(s_mx, 1)

            def max_step(layout, x, n, m0=0, m1=HM, first=False):
                m = rowmax[:, m0:m1, :].rearrange("p m t -> p t m")
                p1, p2, p3 = [mparts[:, :, a, m0:m1] for a in range(PARTS)]
                r1, r2 = [mres[:, :, a, m0:m1] for a in range(PARTS - 1)]
                if n == 0:
                    if first:
                        dve.wait_ge(s_pad, 1)
                    else:
                        dve.wait_ge(s_mT, layout)
                    dve.wait_ge(s_mx, UNITS * x + 2 * m1)
                    V.tensor_scalar(p1, m, -1.0, None, ALU.mult).then_inc(s_ms, 1)
                if n == 1:
                    dve.wait_ge(s_ms, MS_STEPS * layout + 1)
                    V.tensor_tensor(r1, m, p1, ALU.add).then_inc(s_ms, 1)
                if n == 2:
                    dve.wait_ge(s_ms, MS_STEPS * layout + 2)
                    V.tensor_scalar(p2, r1, -1.0, None, ALU.mult).then_inc(s_ms, 1)
                if n == 3:
                    dve.wait_ge(s_ms, MS_STEPS * layout + 3)
                    V.tensor_tensor(r2, r1, p2, ALU.add).then_inc(s_ms, 1)
                if n == 4:
                    dve.wait_ge(s_ms, MS_STEPS * layout + 4)
                    V.tensor_scalar(p3, r2, -1.0, None, ALU.mult).then_inc(s_ms, 1)

            V.memset(ones_b[:, :], 1.0).then_inc(s_ones, 1)
            for n in range(LN_STEPS):
                norm_step(0, n, first=True)
            dve.wait_ge(s_small, 64)
            V.tensor_scalar(omd[:, :], dw_col[:, :], -1.0, 1.0, ALU.mult, ALU.add).then_inc(s_const, 1)
            dve.wait_ge(s_const, 1)
            V.tensor_scalar(ndw[:, :], dw_col[:, :], -1.0, None, ALU.mult).then_inc(s_const, 1)
            dve.wait_ge(s_const, 2)
            V.tensor_tensor(wos[:, :], nw_col[:, :], omd[:, :], ALU.mult).then_inc(s_const, 1)
            dve.wait_ge(s_const, 3)
            V.tensor_tensor(bos[:, :], bo_col[:, :], omd[:, :], ALU.mult).then_inc(s_const, 1)
            dve.wait_ge(s_const, 4)
            dve.wait_ge(s_wTc, 3)
            V.tensor_scalar(woT[:, :], ST[0][:, 3 * P:4 * P], wos[:, 0:1], None, ALU.mult).then_inc(s_woT, 1)
            norm_step(1, 0)
            residue(0, s_q1, s_qr, s_q3, qparts, qres, 2, first=True)
            norm_step(1, 1)
            residue(0, s_k1, s_kr, s_k3, kparts, kres, 0, first=True)
            dve.wait_ge(s_kr, 1)
            V.tensor_copy(kparts[:, 1, :], kres).then_inc(s_k3, 1)
            dve.wait_ge(s_k3, 1)
            V.tensor_tensor(kres, kres, kparts[:, 1, :], ALU.subtract).then_inc(s_k3, 1)
            dve.wait_ge(s_k3, 2)
            V.tensor_copy(kparts[:, 2, :], kres).then_inc(s_k3, 1)
            for n in range(2, LN_STEPS):
                norm_step(1, n)
            for e in range(E):
                last = V.memset(rank[:, :, e:e + 1], float(E - e))
            last.then_inc(s_rank, 1)
            dve.wait_ge(s_rank, 1)
            for u in range(UNITS):
                row_max(0, u)
                if u < TOP_STEPS:
                    top_step(0, u, first=True)
                if u == 5:
                    residue(1, s_q1, s_qr, s_q3, qparts, qres, 2)
                if u == 7:
                    residue(1, s_k1, s_kr, s_k3, kparts, kres, 0)
                if 0 <= u - EARLY_UNIT < MS_STEPS:
                    max_step(0, 0, u - EARLY_UNIT, 0, EARLY, first=True)
            for n in range(MS_STEPS):
                max_step(1, 0, n, EARLY, HM)

            def residual(b):
                dve.wait_ge(s_u, b + 1)
                dve.wait_ge(s_xr, 16 * b + 16)
                V.tensor_tensor(res[:, :, :].rearrange("p t d -> p (t d)"), O[:, :],
                                res[:, :, :].rearrange("p t d -> p (t d)"), ALU.add).then_inc(s_out, 1)

            def attend(b, par, more, behind):
                if more:
                    for u in range(UNITS):
                        row_max(b + 1, u)
                        if behind and u == 1:
                            residual(b - 1)
                        if 4 <= u < 4 + TOP_STEPS:
                            top_step(b + 1, u - 4)
                else:
                    residual(b - 1)
                    for g in range(GROUPS):
                        dve.wait_ge(s_av, TILES * b + 16 * (g + 1))
                        V.tensor_copy(oT[:, g, :], O[:, :]).then_inc(s_oe, 1)

            def unpack_step(b, t, n):
                at = OE_STEPS * b + 4 * t
                o = ST[(2, 0)[t % 2]][:, :].rearrange("p (m c) -> p m c", m=HM)
                if n == 0:
                    dve.wait_ge(s_ot, QT * b + t + 1)
                    V.reciprocal(o_inv[:, :].unsqueeze(2), o[:, :, DH:DH + 1]).then_inc(s_on, 1)
                if n == 1:
                    dve.wait_ge(s_on, at + 1)
                    second = o_inv[:, :].rearrange("p (h i) -> p h i", i=MAPS)[:, :, 1:2]
                    V.tensor_scalar(second, second, ndw[:, 0:1], None, ALU.mult).then_inc(s_on, 1)
                if n == 2:
                    dve.wait_ge(s_on, at + 2)
                    V.tensor_tensor(o_sc[:, :, :], o[:, :, 0:DH], per_tile(o_inv[:, :], DH), ALU.mult).then_inc(s_on, 1)
                if n == 3:
                    dve.wait_ge(s_on, at + 3)
                    both = o_sc[:, :, :].rearrange("p (h i) e -> p h i e", i=MAPS)
                    V.tensor_tensor(o_n[:, t, :].rearrange("p (h e) -> p h e", h=H), both[:, :, 0, :],
                                    both[:, :, 1, :], ALU.add).then_inc(s_on, 1)

            def rms_step(b, n):
                at = OE_STEPS * b + 4 * QT
                if n == 0:
                    dve.wait_ge(s_on, at)
                    V.tensor_tensor(sq[:, :, :], o_n[:, :, :], o_n[:, :, :], ALU.mult).then_inc(s_on, 1)
                if n == 1:
                    dve.wait_ge(s_on, at + 1)
                    V.reduce_sum(o_st[:, 0, :], sq[:, :, :], AX).then_inc(s_on, 1)
                if n == 2:
                    dve.wait_ge(s_on, at + 2)
                    V.tensor_scalar(o_st[:, 1, :], o_st[:, 0, :], 1.0 / D, RMS_EPS, ALU.mult, ALU.add).then_inc(s_on, 1)
                if n == 3:
                    dve.wait_ge(s_on, at + 3)
                    dve.wait_ge(s_rp, b + 1)
                    V.tensor_tensor(o_n[:, :, :], o_n[:, :, :], per_tile(o_st[:, 0, :], D), ALU.mult).then_inc(s_on, 1)

            def rest_hid(b, c):
                dve.wait_ge(s_hh, CH * b + c + 1)
                if c >= 2:
                    dve.wait_ge(s_y, CH * b + c - 1)
                V.tensor_tensor(hl[:, c % 2, :], hid[:, c % NHB, :], hh[:, c % 2, :].bitcast(f32), ALU.subtract)\
                 .then_inc(s_hl, 1)

            def ffn(b, par, more, prep):
                if more:
                    for n in range(MS_STEPS):
                        max_step(b + 2, b + 1, n)
                for c in range(CH):
                    if c >= 2:
                        rest_hid(b, c - 2)
                    dve.wait_ge(s_si, CH * b + c + 1)
                    dve.wait_ge(s_h3, CH * b + c + 1)
                    V.tensor_tensor(hid[:, c % NHB, :], S[c % 2][:, 1, :], sil[:, c % 2, :], ALU.mult)\
                     .then_inc(s_hm, 1)
                    if prep and c == 0:
                        norm_step(b + 2, 0)
                        norm_step(b + 2, 1)
                    if prep and c == 1:
                        norm_step(b + 2, 2)
                        norm_step(b + 2, 3)
                    if c == 2:
                        unpack_step(b, 0, 0)
                    if prep and c == 2:
                        norm_step(b + 2, 4)
                    if c == 2:
                        unpack_step(b, 0, 1)
                    if prep and c == 2:
                        norm_step(b + 2, 5)
                    if c == 3:
                        unpack_step(b, 0, 2)
                        unpack_step(b, 0, 3)
                    if prep and c == 4:
                        norm_step(b + 2, 6)
                    if c in (4, 9, 11):
                        t = {4: 1, 9: 2, 11: 3}[c]
                        unpack_step(b, t, 0)
                        unpack_step(b, t, 1)
                    if c in (5, 10):
                        t = {5: 1, 10: 2}[c]
                        unpack_step(b, t, 2)
                        unpack_step(b, t, 3)
                    if c == 11:
                        unpack_step(b, 3, 2)
                    if c == 12:
                        unpack_step(b, 3, 3)
                        rms_step(b, 0)
                        rms_step(b, 1)
                    if c == 13:
                        rms_step(b, 2)
                    if c == 14:
                        rms_step(b, 3)
                    if prep and c == 7:
                        residue(b + 2, s_q1, s_qr, s_q3, qparts, qres, 2)
                    if prep and c == 8:
                        residue(b + 2, s_k1, s_kr, s_k3, kparts, kres, 0)
                rest_hid(b, CH - 2)
                rest_hid(b, CH - 1)

            batches(dve, attend, ffn)
            residual(BATCH - 1)

        @block.tensor
        def _(pe):
            mm, tr = nc.tensor.matmul, nc.tensor.transpose

            def tiles_T(dst, src, idn, s):
                for t in range(QT):
                    last = tr(dst[:, t * P:(t + 1) * P], src(t), idn)
                last.then_inc(s, 1)

            def do_xT(x, bank):
                pe.wait_ge(s_ln, LN_STEPS * x + LN_STEPS)
                tiles_T(ST[bank][:, :], lambda t: xn[:, t, :], ident[:, :], s_xT)

            def project(x, j, bank, s):
                pe.wait_ge(s_xTc, x + 1)
                mm(ST[bank][:, :], wqkvT[:, j, :], xT[:, :], start=True, stop=True).then_inc(s, 1)

            def do_v(x, bank):
                for t in range(QT):
                    last = mm(ST[bank][:, t * P:(t + 1) * P], xT[:, t * P:(t + 1) * P], wqkvT[:, 2, :],
                              start=True, stop=True)
                last.then_inc(s_v, 1)

            def do_g(x, bank):
                for t in range(QT):
                    last = mm(ST[bank][:, t * E:(t + 1) * E], xT[:, t * P:(t + 1) * P], wg[:, :],
                              start=True, stop=True)
                last.then_inc(s_g, 1)

            def do_rwT(x, bank=0):
                pe.wait_ge(s_tk, TOP_STEPS * x + TOP_STEPS)
                tiles_T(ST[bank][0:E, :], lambda t: rw[:, t, :], ident[:, :], s_rwT)

            def do_mT(n, bank):
                pe.wait_ge(s_ms, MS_STEPS * n + MS_STEPS)
                tiles_T(bank[:, 0:SEQ // 2].bitcast(bf16), lambda t: mpad[:, t, :], ident_b[:, :], s_mT)

            def score_unit(x, par, u, half, first=False):
                if half == 0 and (u >= 2 or not first):
                    pe.wait_ge(s_mx, UNITS * x + u - 1)
                t = u % 2 * 2 + half
                ins = mm(S[u % 2][:, half, :], qop[par][0:TERMS, u // 2, t * P:(t + 1) * P],
                         kop[par][0:TERMS, u // 2, :], start=True, stop=True)
                if half == 1:
                    ins.then_inc(s_s, 1)

            def keep_busy(n):
                for _ in range(n):
                    mm(O[:, 0:P], ident_b[:, :], ident_b[:, :], start=True, stop=True)

            pe.wait_ge(s_id, 4)
            keep_busy(BUSY_ID)
            pe.wait_ge(s_wraw, 64)
            for j in range(4):
                last = tr(ST[0][:, j * P:(j + 1) * P], w_raw[:, j, :], ident[:, :])
            last.then_inc(s_wT, 1)
            keep_busy(BUSY_W)
            do_xT(0, 1)
            pe.wait_ge(s_wTc, 3)
            project(0, 0, 2, s_q)
            pe.wait_ge(s_woT, 1)
            project(0, 1, 0, s_k)
            do_v(0, 1)
            pe.wait_ge(s_small, 64)
            pe.wait_ge(s_qr, 1)
            do_g(0, 2)
            pe.wait_ge(s_ql[0], q_rows(0, 0))
            pe.wait_ge(s_kl[0], k_rows(0, 0))
            pe.wait_ge(s_k0, 16 * PARTS)
            for u in range(UNITS):
                for half in range(2):
                    score_unit(0, 0, u, half, first=True)
                if u == 1:
                    pe.wait_ge(s_vc, 1)
                    do_xT(1, 1)
                if u == 3:
                    pe.wait_ge(s_z, 1)
                    project(1, 0, 2, s_q)
                if u == 5:
                    pe.wait_ge(s_kr, 1)
                    project(1, 1, 0, s_k)
                if u == 7:
                    do_v(1, 1)
                if u == 9:
                    pe.wait_ge(s_qr, 2)
                    do_g(1, 2)
                if u == TOP_STEPS + 2:
                    pe.wait_ge(s_vc, 2)
                    do_rwT(0, 1)
                if u == EARLY_UNIT + MS_STEPS + 1:
                    pe.wait_ge(s_kr, 2)
                    do_mT(0, ST[0])

            def finish(b):
                pe.wait_ge(s_yc, b + 1)
                tiles_T(O[:, :], lambda t: yT[:, t * P:(t + 1) * P], ident[:, :], s_u)

            def score_tile(b, par, s, more):
                banks = score_banks(more)
                if s == 0:
                    pe.wait_ge(s_rwc, b + 1)
                if s == 0 and more:
                    pe.wait_ge(s_vc, b + 2)
                    pe.wait_ge(s_z, b + 2)
                if s >= len(banks):
                    pe.wait_ge(s_p, TILES * b + s + 1 - len(banks))
                m, t = s // (4 * QT) * 4 + s % 4, s // 4 % QT
                mm(banks[s % len(banks)], kop[par][:, m, t * P:(t + 1) * P], qop[par][:, m, :],
                   start=True, stop=True).then_inc(s_st, 1)
                if more:
                    score_unit(b + 1, 1 - par, s // 2, s % 2)

            def start_attend(b, par, more, behind, s):
                if s == 0:
                    pe.wait_ge(s_kone, 32)
                    pe.wait_ge(s_ml, MD * b + (2 * MD if behind else MD))
                    if more:
                        pe.wait_ge(s_ql[1 - par], q_rows(b + 1, 1 - par))
                        pe.wait_ge(s_kl[1 - par], k_rows(b + 1, 1 - par))
                score_tile(b, par, s, more)

            def attend(b, par, more, behind):
                pe.wait_ge(s_vc, b + 1)
                if not behind:
                    for s in range(3):
                        start_attend(b, par, more, behind, s)
                for quad in range(GROUPS * QT + 1):
                    if quad < GROUPS * QT:
                        for s in range(4 * quad, 4 * quad + 4):
                            if not behind and s == EARLY * QT:
                                pe.wait_ge(s_ml, 2 * MD)
                            if s >= 3:
                                score_tile(b, par, s, more)
                            if s == FINISH and behind:
                                finish(b - 1)
                    if quad == 0 and not behind:
                        do_mT(1, O)
                    if quad:
                        g, t = divmod(quad - 1, QT)
                        if quad == 1 and behind:
                            pe.wait_ge(s_out, b)
                        if quad == 1 and not behind:
                            pe.wait_ge(s_mc, 2)
                        if t == 0 and g:
                            pe.wait_ge(s_oe, GROUPS * b + g)
                        for j in range(4):
                            s = 4 * (quad - 1) + j
                            pe.wait_ge(s_p, TILES * b + s + 1)
                            mm(O[VW * j:VW * (j + 1), :], vop[par][:, t, (4 * g + j) // MAPS, :],
                               probs[:, s % NP, :], start=(t == 0), stop=(t == QT - 1),
                               tile_position=(0, VW * j)).then_inc(s_av, 1)

            def do_oT(b, t, bank):
                for g in range(GROUPS):
                    last = tr(ST[bank][:, g * P:(g + 1) * P], oT[:, g, t * P:(t + 1) * P], ident[:, :])
                last.then_inc(s_ot, 1)

            def down(b, c, last=False):
                pe.wait_ge(s_hl, CH * b + c + 1)
                wh, wl = w2h[:, c // FC, c % FC, :], w2l[:, c // FC, c % FC, :]
                mm(O[:, :], wh, hh[:, c % 2, :], start=(c == 0), stop=False)
                mm(O[:, :], wh, hl[:, c % 2, :], start=False, stop=False)
                mm(O[:, :], wl, hh[:, c % 2, :], start=False, stop=last).then_inc(s_y, 1)

            def ffn(b, par, more, prep):
                pe.wait_ge(s_p, TILES * (b + 1))
                pe.wait_ge(s_xs, 2 * b + 2)
                pe.wait_ge(s_w13, 2 * (E + SHARED))
                pe.wait_ge(s_w2s, 3)
                for c in range(CH):
                    if more and c < 2:
                        pe.wait_ge(s_mx, UNITS * (b + 2) - 1 + c)
                    if c >= 2:
                        pe.wait_ge(s_hm, CH * b + c - 1)
                    for side, s in ((0, s_h1), (1, s_h3)):
                        at = slice(side * FF + c % FC * P, side * FF + c % FC * P + P)
                        dst = S[c % 2][:, side, :]
                        mm(dst, w13h[:, c // FC, at], xh[par][:, :], start=True, stop=False)
                        mm(dst, w13h[:, c // FC, at], xl[par][:, :], start=False, stop=False)
                        mm(dst, w13l[:, c // FC, at], xh[par][:, :], start=False, stop=True).then_inc(s, 1)
                    if c >= LAG:
                        down(b, c - LAG)
                    if more and c == 0:
                        do_rwT(b + 1)
                    if c == 1:
                        pe.wait_ge(s_oe, GROUPS * (b + 1))
                        do_oT(b, 0, 2)
                    if more and c == 2:
                        do_mT(b + 2, ST[1])
                    if c == 3:
                        if more:
                            pe.wait_ge(s_rwc, b + 2)
                        do_oT(b, 1, 0)
                    if prep:
                        x = b + 2
                        if c == 5:
                            pe.wait_ge(s_mc, b + 3)
                            do_xT(x, 1)
                        if c == 6:
                            pe.wait_ge(s_on, OE_STEPS * b + 4)
                            project(x, 0, 2, s_q)
                        if c == 7:
                            pe.wait_ge(s_on, OE_STEPS * b + 8)
                            project(x, 1, 0, s_k)
                        if c == 9:
                            do_v(x, 1)
                        if c == 11:
                            pe.wait_ge(s_vc, x + 1)
                            do_g(x, 1)
                    if c == 8:
                        pe.wait_ge(s_on, OE_STEPS * b + 4)
                        if prep:
                            pe.wait_ge(s_qr, b + 3)
                        do_oT(b, 2, 2)
                    if c == 10:
                        pe.wait_ge(s_on, OE_STEPS * b + 8)
                        if prep:
                            pe.wait_ge(s_kr, b + 3)
                        do_oT(b, 3, 0)
                    if c == 16:
                        pe.wait_ge(s_on, OE_STEPS * (b + 1))
                        tiles_T(ST[2][:, :], lambda t: o_n[:, t, :], ident[:, :], s_nT)
                for c in range(CH - LAG, CH):
                    if more:
                        s = c - CH + LAG
                        if s < 2 and prep:
                            pe.wait_ge(s_hm, CH * (b + 1) - 1)
                        if s == 2:
                            pe.wait_ge(s_nc, b + 1)
                            pe.wait_ge(s_hm, CH * (b + 1))
                        start_attend(b + 1, 1 - par, prep, True, s)
                    if c == CH - 1:
                        pe.wait_ge(s_nc, b + 1)
                        mm(O[:, :], woT[:, :], nT[:, :], start=False, stop=False)
                    down(b, c, last=c == CH - 1)

            batches(pe, attend, ffn)
            finish(BATCH - 1)


_INS = ['L0_attn_x', 'L0_attn_Wq', 'L0_attn_Wk', 'L0_attn_Wv', 'L0_attn_norm_w', 'L0_attn_Wo', 'L0_attn_bo',
        'L0_attn_diff_weight', 'L0_ffn_Wg', 'L0_ffn_Ws1', 'L0_ffn_Ws3', 'L0_ffn_Ws2', 'L0_ffn_We1', 'L0_ffn_We3',
        'L0_ffn_We2']


def kernel(**inputs):
    import numpy as np
    import concourse.bacc as bacc
    from concourse.bass_utils import run_bass_kernel_spmd

    nc = bacc.Bacc("TRN2", target_bir_lowering=False, num_devices=1)
    arrays, args = {}, []
    for name in _INS:
        a = np.ascontiguousarray(inputs[name])
        if a.ndim == 0:
            a = a.reshape(1)
        arrays[f"in_{name}"] = a
        args.append(nc.dram_tensor(f"in_{name}", a.shape, mybir.dt.from_np(a.dtype), kind="ExternalInput").ap())
    shape = inputs['L0_attn_x'].shape
    args.append(nc.dram_tensor("out_x", shape, mybir.dt.float32, kind="ExternalOutput").ap())
    differential_attention_moe_block(nc, *args)
    r = run_bass_kernel_spmd(nc, [arrays], core_ids=[0])
    return r.results[0]["out_x"]
```
